# Optimizing a Trainium2 kernel written in Bass

```python
import numpy as np
import jax
import jax.numpy as jnp

def _softmax(x, axis=-1):
    return jax.nn.softmax(x, axis=axis)

def _gelu(x):
    return jax.nn.gelu(x, approximate=True)

def _silu(x):
    return jax.nn.silu(x)

def _sigmoid(x):
    return jax.nn.sigmoid(x)

def _layernorm(x, axis=-1, eps=1e-05):
    m = jnp.mean(x, axis=axis, keepdims=True)
    v = jnp.var(x, axis=axis, keepdims=True)
    return (x - m) / jnp.sqrt(v + eps)

def _scatter_add(tgt, idx, src, axis=0):
    return tgt.at[idx].add(src)

def _segment_sum(src, seg, n):
    return jax.ops.segment_sum(src, seg, n)
kernel_name = 'mk_gnn_preln_d2_gnn_r8_94b1e1'

def setup_inputs(seed: int=0):
    np.random.seed(seed)
    _w = jnp.asarray

    def _rec_inputs():
        import jax
        import jax.numpy as jnp
        _gk = jax.random.key(seed)
        x = -0.0003713 + 1 * jax.random.normal(jax.random.fold_in(_gk, 1), (6250, 256), jnp.float32)
        src = jax.random.randint(jax.random.fold_in(_gk, 2), (200000,), 0, 6250, jnp.int32)
        dst = jnp.minimum((6250 * jax.random.uniform(jax.random.fold_in(_gk, 3), (200000,)) ** 2.0).astype(jnp.int32), 49999)
        _o = jnp.argsort(dst, stable=True)
        src = src[_o]
        dst = dst[_o]
        return (x, src, dst)
    x, src, dst = _rec_inputs()

    def _L0_gnn_setup():
        import jax, jax.numpy as jnp
        import numpy as np
        N, F, H, D = (6250, 256, 4, 64)
        E = 100000
        LN_EPS = 1e-05

        def _layernorm(x, g, b):
            mu = jnp.mean(x, axis=-1, keepdims=True)
            var = jnp.mean(jnp.square(x - mu), axis=-1, keepdims=True)
            return (x - mu) * jax.lax.rsqrt(var + LN_EPS) * g + b
        key = jax.random.key(seed)
        ks = jax.random.split(key, 12)
        s = 1.0 / np.sqrt(F)
        return {'feat': jax.random.normal(ks[0], (N, F), dtype=jnp.float32), 'src': jax.random.randint(ks[1], (E,), 0, N, dtype=jnp.int32), 'dst': jax.random.randint(ks[2], (E,), 0, N, dtype=jnp.int32), 'Wq': jax.random.uniform(ks[3], (F, H * D), jnp.float32, -s, s), 'Wk': jax.random.uniform(ks[4], (F, H * D), jnp.float32, -s, s), 'Wv': jax.random.uniform(ks[5], (F, H * D), jnp.float32, -s, s), 'ln_g': jnp.ones((F,), jnp.float32), 'ln_b': jnp.zeros((F,), jnp.float32), 'W1': jax.random.uniform(ks[6], (F, 4 * F), jnp.float32, -s, s), 'b1': jnp.zeros((4 * F,), jnp.float32), 'alpha': jnp.full((4 * F,), 0.25, jnp.float32), 'W2': jax.random.uniform(ks[7], (4 * F, F), jnp.float32, -s / 2.0, s / 2.0), 'b2': jnp.zeros((F,), jnp.float32)}
    _L0_gnn_all = _L0_gnn_setup()
    _L0_gnn_in = {k: v for k, v in _L0_gnn_all.items() if k in ('Wq', 'Wk', 'Wv', 'ln_g', 'ln_b', 'W1', 'b1', 'alpha', 'W2', 'b2')}
    del _L0_gnn_all

    def _L1_gnn_setup():
        import jax, jax.numpy as jnp
        import numpy as np
        N, IN_CH, HEADS, OUT_CH, E = (6250, 256, 4, 64, 100000)
        key = jax.random.key(seed)
        k1, k2, k3, k4, k5 = jax.random.split(key, 5)
        x = jax.random.normal(k1, (N, IN_CH), dtype=jnp.float32)
        edge_index = jax.random.randint(k2, (2, E), 0, N, dtype=jnp.int64)
        bw = float(np.sqrt(6.0 / (IN_CH + HEADS * OUT_CH)))
        ba = float(np.sqrt(6.0 / (HEADS + OUT_CH)))
        weight = jax.random.uniform(k3, (IN_CH, HEADS * OUT_CH), jnp.float32, -bw, bw)
        attn_l = jax.random.uniform(k4, (HEADS, OUT_CH), jnp.float32, -ba, ba)
        attn_r = jax.random.uniform(k5, (HEADS, OUT_CH), jnp.float32, -ba, ba)
        return {'x': x, 'edge_index': edge_index, 'weight': weight, 'attn_l': attn_l, 'attn_r': attn_r}
    _L1_gnn_all = _L1_gnn_setup()
    _L1_gnn_in = {k: v for k, v in _L1_gnn_all.items() if k in ('weight', 'attn_l', 'attn_r')}
    del _L1_gnn_all
    return {'x': x, 'src': src, 'dst': dst, 'L0_gnn_Wq': _L0_gnn_in['Wq'], 'L0_gnn_Wk': _L0_gnn_in['Wk'], 'L0_gnn_Wv': _L0_gnn_in['Wv'], 'L0_gnn_ln_g': _L0_gnn_in['ln_g'], 'L0_gnn_ln_b': _L0_gnn_in['ln_b'], 'L0_gnn_W1': _L0_gnn_in['W1'], 'L0_gnn_b1': _L0_gnn_in['b1'], 'L0_gnn_alpha': _L0_gnn_in['alpha'], 'L0_gnn_W2': _L0_gnn_in['W2'], 'L0_gnn_b2': _L0_gnn_in['b2'], 'L1_gnn_weight': _L1_gnn_in['weight'], 'L1_gnn_attn_l': _L1_gnn_in['attn_l'], 'L1_gnn_attn_r': _L1_gnn_in['attn_r']}

def reference(x, src, dst, L0_gnn_Wq, L0_gnn_Wk, L0_gnn_Wv, L0_gnn_ln_g, L0_gnn_ln_b, L0_gnn_W1, L0_gnn_b1, L0_gnn_alpha, L0_gnn_W2, L0_gnn_b2, L1_gnn_weight, L1_gnn_attn_l, L1_gnn_attn_r):
    import jax
    import jax.numpy as jnp

    def _L0_gnn_ref(feat, src, dst, Wq, Wk, Wv, ln_g, ln_b, W1, b1, alpha, W2, b2):
        import jax, jax.numpy as jnp
        import numpy as np
        N, F, H, D = (6250, 256, 4, 64)
        E = 100000
        LN_EPS = 1e-05

        def _layernorm(x, g, b):
            mu = jnp.mean(x, axis=-1, keepdims=True)
            var = jnp.mean(jnp.square(x - mu), axis=-1, keepdims=True)
            return (x - mu) * jax.lax.rsqrt(var + LN_EPS) * g + b
        feat_c = jax.lax.stop_gradient(feat)
        q = (feat @ Wq).reshape(N, H, D)
        k = (feat_c @ Wk).reshape(N, H, D)
        v = (feat_c @ Wv).reshape(N, H, D)
        e = jnp.einsum('ehd,ehd->eh', k[src], q[dst]) / jnp.sqrt(jnp.float32(H * D))
        emax = jax.ops.segment_max(e, dst, num_segments=N)
        ex = jnp.exp(e - emax[dst])
        denom = jax.ops.segment_sum(ex, dst, num_segments=N)
        a = ex / denom[dst]
        m = v[src] * a[..., None]
        ft2 = jax.ops.segment_sum(m, dst, num_segments=N).reshape(N, F)
        rst = ft2 + feat
        rst = _layernorm(rst, ln_g, ln_b)
        h = rst @ W1 + b1
        h = jnp.where(h > 0, h, alpha * h)
        ffn = h @ W2 + b2
        rst = _layernorm(rst + ffn, ln_g, ln_b)
        return rst

    def _L1_gnn_ref(x, edge_index, weight, attn_l, attn_r):
        import jax, jax.numpy as jnp
        import numpy as np
        N, IN_CH, HEADS, OUT_CH, E = (6250, 256, 4, 64, 100000)
        heads, out_ch = attn_l.shape
        n = x.shape[0]
        xt = jnp.matmul(x, weight).reshape(-1, heads, out_ch)
        row, col = (edge_index[0], edge_index[1])
        alpha_l = jnp.einsum('ehd,hd->eh', xt[row], attn_l)
        alpha_r = jnp.einsum('ehd,hd->eh', xt[col], attn_r)
        alpha = jax.nn.softmax(jax.nn.leaky_relu(alpha_l + alpha_r, 0.01), axis=1)
        tmp = jnp.einsum('nh,nhd->nd', alpha[:n], xt[col[:n]])
        out = jnp.broadcast_to(tmp[:, None, :], (n, heads, out_ch))
        return out.reshape(n, heads * out_ch)
    edge_index = jnp.stack([src, dst])
    h = jnp.maximum(_layernorm(x, axis=-1), 0.0)
    x = x + _L0_gnn_ref(h, src, dst, L0_gnn_Wq, L0_gnn_Wk, L0_gnn_Wv, L0_gnn_ln_g, L0_gnn_ln_b, L0_gnn_W1, L0_gnn_b1, L0_gnn_alpha, L0_gnn_W2, L0_gnn_b2)
    h = jnp.maximum(_layernorm(x, axis=-1), 0.0)
    x = x + _L1_gnn_ref(h, edge_index, L1_gnn_weight, L1_gnn_attn_l, L1_gnn_attn_r)
    return x

_drawn_inputs = setup_inputs


def setup_inputs(seed=0):
    import zlib

    import numpy as np

    out = dict(_drawn_inputs(seed))
    spreads = {'L0_gnn_ln_g': (1.0, 0.2),
     'L0_gnn_ln_b': (0.0, 0.1),
     'L0_gnn_b1': (0.0, 0.382),
     'L0_gnn_alpha': (0.25, 0.6),
     'L0_gnn_b2': (0.0, 0.1)}
    factors = {'L0_gnn_Wq': 8.0, 'L0_gnn_Wk': 8.0}
    for name, (base, spread) in spreads.items():
        noise = np.random.default_rng([zlib.crc32(name.encode()), seed]).standard_normal(out[name].shape)
        drawn = base * np.exp(spread * noise) if base else spread * noise
        out[name] = jnp.asarray(drawn.astype(out[name].dtype))
    for name, factor in factors.items():
        out[name] = (out[name] * factor).astype(out[name].dtype)
    return out
```

```python
import concourse.bass as bass
from concourse import mybir
from contextlib import ExitStack

fp32 = mybir.dt.float32
i32 = mybir.dt.int32
i16 = mybir.dt.int16
ALU = mybir.AluOpType
ACT = mybir.ActivationFunctionType
AX = mybir.AxisListType.X

P = 128
N, F = 6250, 256
H, D = 4, 64
HID = 4 * F
E = 200000
NT = -(-N // P)
TAIL = N - (NT - 1) * P
NTE = NT + 1
G = 4
EG = G * P
NG = -(-E // EG)
NROW = NG * G
NCH = -(-NROW // P)
NS = NG + NT - 1
W = D + 1
U = 4
BIG = 2.0 ** 100
PAD_DST = 8191
EPS = 1e-5
SCALE = 1.0 / 16.0


class Names:
    pass


def carve(arena, at, shape, dt=fp32):
    size = 1
    for n in shape[1:]:
        size *= n
    v = arena[0:shape[0], at:at + size]
    if dt is not fp32:
        v = v.bitcast(dt)
    if len(shape) == 3:
        v = v.rearrange("p (a b) -> p a b", b=shape[2])
    if len(shape) == 4:
        v = v.rearrange("p (a b c) -> p a b c", b=shape[2], c=shape[3])
    return v


def wait(eng, sem, value):
    if isinstance(value, int) and value <= 0:
        return
    eng.wait_ge(sem, value)


def bcast(ap, axis, n):
    shape = list(ap.shape)
    shape[axis] = n
    return ap.broadcast_to(shape)


def gnn_kernel(nc, x, src, dst, Wq, Wk, Wv, ln_g, ln_b, W1, b1, alpha, W2, b2, weight, attn_l, attn_r, out):
    kv_tab = nc.dram_tensor("kv_tab", (NT * P, 2 * F), fp32, kind="Internal").ap()
    h_tab = nc.dram_tensor("h_tab", (NT * P, F), fp32, kind="Internal").ap()
    xt_tab = nc.dram_tensor("xt_tab", (NT * P, F + H), fp32, kind="Internal").ap()
    al_tab = nc.dram_tensor("al_tab", (NT * P, H), fp32, kind="Internal").ap()
    dst_pad = nc.dram_tensor("dst_pad", (NROW * P,), i16, kind="Internal").ap()
    flag_tab = nc.dram_tensor("flag_tab", (NROW, P), fp32, kind="Internal").ap()
    meta_tab = nc.dram_tensor("meta_tab", (P, NG * 3 * G), fp32, kind="Internal").ap()
    T = Names()
    T.x, T.src, T.dst, T.out = x, src, dst, out
    T.Wq, T.Wk, T.Wv, T.ln_g, T.ln_b = Wq, Wk, Wv, ln_g, ln_b
    T.W1, T.b1, T.alpha, T.W2, T.b2 = W1, b1, alpha, W2, b2
    T.weight, T.attn_l, T.attn_r = weight, attn_l, attn_r
    T.kv_tab, T.h_tab, T.xt_tab, T.al_tab = kv_tab, h_tab, xt_tab, al_tab
    T.dst_pad, T.flag_tab, T.meta_tab = dst_pad, flag_tab, meta_tab
    with ExitStack() as ctx:
        T.arena = ctx.enter_context(nc.sbuf_tensor("arena", [P, 52600], fp32))
        T.psum = ctx.enter_context(nc.psum_tensor("psum", [P, 8, 512], fp32))
        c = Names()
        at = 0

        def keep(shape, dt=fp32):
            nonlocal at
            size = 1
            for n in shape[1:]:
                size *= n
            at += size
            return carve(T.arena, at - size, shape, dt)
        c.acc = keep([P, NTE * H * W])
        c.ident = keep([P, P])
        c.win_nodes = keep([P, NS])
        c.nt_row = keep([1, NS + 1], i32)
        c.ea_row = keep([1, NS + 1], i32)
        c.win_base = keep([P, NS])
        c.win_new = keep([P, NS])
        c.iota = keep([P, EG])
        c.base = at
        T.c = c
        schedule_phase(nc, T)
        feature_phase(nc, T)
        edge_phase(nc, T)
        node_phase(nc, T)
        output_phase(nc, T)


def schedule_phase(nc, T):
    c = T.c
    at = c.base
    dst_i = carve(T.arena, at, [P, NCH, P], i32); at += NCH * P
    src_i = carve(T.arena, at, [P, NCH, P], i32); at += NCH * P
    dst_s = carve(T.arena, at, [P, NCH * P // 2]).bitcast(i16).rearrange("p (c f) -> p c f", f=P); at += NCH * P // 2
    dst_f = carve(T.arena, at, [P, NCH, P]); at += NCH * P
    src_f = carve(T.arena, at, [P, NCH, P]); at += NCH * P
    start = carve(T.arena, at, [P, NCH, P]); at += NCH * P
    end = carve(T.arena, at, [P, NCH, P]); at += NCH * P
    meta = carve(T.arena, at, [P, NCH * P // G, 3 * G]); at += NCH * P * 3
    meta_i = meta.bitcast(i32)
    last = carve(T.arena, at, [NT - 1, NG, 3 * G]); at += NG * 3 * G
    less = carve(T.arena, at, [NT - 1, NG]); at += NG
    iota_row = c.iota[:, 0:P]
    part = carve(T.arena, at, [P, 1]); at += 1
    limit = carve(T.arena, at, [P, 1]); at += 1
    turn = carve(T.arena, at, [P, 1]); at += 1
    reach = carve(T.arena, at, [NT - 1, NS]); at += NS
    ones = carve(T.arena, at, [NT - 1, P]); at += P
    nt_f = carve(T.arena, at, [P, NS]); at += NS
    ea_f = carve(T.arena, at, [1, NS]); at += NS
    ps = T.psum
    full = E // P
    rows_last = NROW - (NCH - 1) * P
    full_last = full - (NCH - 1) * P
    rest = E - full * P
    with ExitStack() as ctx:
        def sem(name):
            return ctx.enter_context(nc.semaphore(name))
        shorts_set = sem("shorts_set")
        pads_set, edges_in, padded_out, iotas = sem("pads_set"), sem("edges_in"), sem("padded_out"), sem("iotas")
        dve, transposed, meta_built, meta_out, last_in = sem("sdve"), sem("transposed"), sem("meta_built"), sem("meta_out"), sem("last_in")
        consts, nt_counted, reached, flags_set, flags_out = sem("consts"), sem("nt_counted"), sem("reached"), sem("flags_set"), sem("flags_out")
        block = ctx.enter_context(nc.Block())

        @block.sync
        def _(sp):
            sp.wait_ge(pads_set, 2)
            for lst, tile in ((T.dst, dst_i), (T.src, src_i)):
                sp.dma_start(tile[:, 0:NCH - 1, :], lst[0:(NCH - 1) * P * P].rearrange("(c p f) -> p c f", p=P, f=P)).then_inc(edges_in, 16)
                sp.dma_start(tile[0:full_last, NCH - 1, :], lst[(NCH - 1) * P * P:full * P].rearrange("(p f) -> p f", f=P)).then_inc(edges_in, 16)
                sp.dma_start(tile[full_last:full_last + 1, NCH - 1, 0:rest], lst[full * P:E].unsqueeze(0)).then_inc(edges_in, 16)
            sp.wait_ge(shorts_set, 1)
            sp.dma_start(T.dst_pad[0:(NCH - 1) * P * P].rearrange("(c p f) -> p c f", p=P, f=P), dst_s[:, 0:NCH - 1, :]).then_inc(padded_out, 16)
            sp.dma_start(T.dst_pad[(NCH - 1) * P * P:NROW * P].rearrange("(p f) -> p f", f=P), dst_s[0:rows_last, NCH - 1, :]).then_inc(padded_out, 16)
            sp.wait_ge(flags_set, 1)
            sp.dma_start(T.flag_tab[0:(NCH - 1) * P, :].rearrange("(c p) f -> p c f", p=P), start[:, 0:NCH - 1, :]).then_inc(flags_out, 16)
            sp.dma_start(T.flag_tab[(NCH - 1) * P:NROW, :], start[0:rows_last, NCH - 1, :]).then_inc(flags_out, 16)
            sp.wait_ge(meta_built, 3 * NCH)
            sp.dma_start(T.meta_tab[:, :], meta[:, 0:NG, :].rearrange("p a b -> p (a b)")).then_inc(meta_out, 16)
            sp.wait_ge(meta_out, 16)
            sp.dma_start(last[:, :, :].rearrange("p a b -> p (a b)"), T.meta_tab[P - 1:P, :].broadcast_to([NT - 1, NG * 3 * G])).then_inc(last_in, 16)
            sp.wait_ge(padded_out, 32)
            sp.wait_ge(flags_out, 32)

        @block.gpsimd
        def _(pool):
            nc.gpsimd.iota(c.iota[:, :], pattern=[[1, EG]], base=0, channel_multiplier=0,
                           allow_small_or_imprecise_dtypes=True).then_inc(iotas, 1)
            nc.gpsimd.iota(part[:, :], pattern=[[0, 1]], base=0, channel_multiplier=1,
                           allow_small_or_imprecise_dtypes=True).then_inc(iotas, 1)

        @block.vector
        def _(v):
            done = [0]

            def link(ins):
                done[0] += 1
                ins.then_inc(dve, 1)
                v.wait_ge(dve, done[0])
            nc.vector.memset(dst_i[:, NCH - 1, :], PAD_DST).then_inc(pads_set, 1)
            nc.vector.memset(src_i[:, NCH - 1, :], 0).then_inc(pads_set, 1)
            nc.vector.memset(start[:, :, 0:1], 0.0)
            nc.vector.memset(end[:, :, P - 1:P], 1.0)
            nc.vector.memset(ones[:, :], 1.0)
            v.wait_ge(iotas, 2)
            nc.vector.tensor_scalar(c.ident[:, :], iota_row, part[:, 0:1], None, ALU.is_equal).then_inc(consts, 1)
            link(nc.vector.tensor_scalar(limit[:, :], part[:, :], 1.0, float(P), ALU.add, ALU.mult))
            v.wait_ge(edges_in, 6 * 16)
            nc.vector.tensor_copy(dst_s[:, :, :], dst_i[:, :, :]).then_inc(shorts_set, 1)
            link(nc.vector.tensor_copy(dst_f[:, :, :], dst_i[:, :, :]))
            link(nc.vector.tensor_copy(src_f[:, :, :], src_i[:, :, :]))
            link(nc.vector.tensor_tensor(end[:, :, 0:P - 1], dst_f[:, :, 1:P], dst_f[:, :, 0:P - 1], ALU.not_equal))
            nc.vector.tensor_scalar(start[:, :, 1:P], end[:, :, 0:P - 1], -BIG, None, ALU.mult).then_inc(flags_set, 1)
            for k in range(NCH):
                v.wait_ge(transposed, k + 1)
                rows = slice(k * P // G, (k + 1) * P // G)
                bank = ps[:, k % 2, 0:3 * P].rearrange("p (w a t) -> p w a t", w=3, t=G)
                nc.vector.tensor_copy(meta_i[:, rows, 0:G], bank[:, 0]).then_inc(meta_built, 1)
                nc.vector.tensor_copy(meta[:, rows, G:2 * G], bank[:, 1]).then_inc(meta_built, 1)
                nc.vector.tensor_copy(meta[:, rows, 2 * G:3 * G], bank[:, 2]).then_inc(meta_built, 1)
            v.wait_ge(last_in, 16)
            link(nc.vector.tensor_scalar(less[:, :], last[:, :, 2 * G - 1], limit[0:NT - 1, 0:1], None, ALU.is_lt))
            link(nc.vector.tensor_reduce(turn[0:NT - 1, :], less[:, :], AX, ALU.add))
            link(nc.vector.tensor_scalar(turn[0:NT - 1, :], turn[0:NT - 1, :], part[0:NT - 1, 0:1], 1.0, ALU.add, ALU.add))
            nc.vector.tensor_scalar(reach[:, :], c.iota[0:NT - 1, 0:NS], turn[0:NT - 1, 0:1], None, ALU.is_ge).then_inc(reached, 1)
            v.wait_ge(nt_counted, 1)
            link(nc.vector.tensor_copy(nt_f[:, :], ps[:, 2, 0:NS]))
            link(nc.vector.tensor_scalar(c.win_base[:, :], nt_f[:, :], float(P), None, ALU.mult))
            link(nc.vector.memset(c.win_new[:, 0:1], 0.0))
            link(nc.vector.tensor_tensor(c.win_new[:, 1:NS], nt_f[:, 1:NS], nt_f[:, 0:NS - 1], ALU.not_equal))
            link(nc.vector.tensor_scalar(c.win_new[:, 1:NS], c.win_new[:, 1:NS], -2.0 * BIG, None, ALU.mult))
            link(nc.vector.tensor_scalar(c.win_nodes[:, :], nt_f[:, :], float(P), part[:, 0:1], ALU.mult, ALU.add))
            link(nc.vector.tensor_copy(c.nt_row[0:1, 0:NS], nt_f[0:1, :]))
            link(nc.vector.tensor_tensor(ea_f[:, :], c.iota[0:1, 0:NS], nt_f[0:1, :], ALU.subtract))
            link(nc.vector.tensor_copy(c.ea_row[0:1, 0:NS], ea_f[:, :]))

        @block.tensor
        def _(pe):
            pe.wait_ge(consts, 1)
            pe.wait_ge(flags_set, 1)
            for k in range(NCH):
                if k >= 2:
                    pe.wait_ge(meta_built, 3 * (k - 1))
                for w, tile in enumerate((src_f, dst_f, end)):
                    t = nc.tensor.transpose(ps[:, k % 2, w * P:(w + 1) * P], tile[:, k, :], c.ident[:, :])
                t.then_inc(transposed, 1)
            pe.wait_ge(reached, 1)
            nc.tensor.matmul(ps[:, 2, 0:NS], ones[:, :], reach[:, :], start=True, stop=True).then_inc(nt_counted, 1)


def feature_phase(nc, T):
    c = T.c
    at = c.base
    c.q = carve(T.arena, at, [P, NTE, F]); at += NTE * F
    wall = carve(T.arena, at, [P, 2, 3 * F]); at += 6 * F
    hT = carve(T.arena, at, [P, 2, F]); at += 2 * F
    kv = carve(T.arena, at, [P, 2, 2 * F]); at += 4 * F
    hs = carve(T.arena, at, [P, 2, F]); at += 2 * F
    stats = carve(T.arena, at, [P, NT, 6]); at += NT * 6
    half = carve(T.arena, at, [P, NT]); at += NT
    mean = carve(T.arena, at, [P, NT]); at += NT
    var = carve(T.arena, at, [P, NT]); at += NT
    rstd = carve(T.arena, at, [P, NT]); at += NT
    std = carve(T.arena, at, [P, NT]); at += NT
    nmr = carve(T.arena, at, [P, NT]); at += NT
    X = c.acc[:, 0:NT * F].rearrange("p (t f) -> p t f", f=F)
    ps = T.psum
    LOADS = 4
    PER = (NT - 1) // LOADS
    with ExitStack() as ctx:
        def sem(name):
            return ctx.enter_context(nc.semaphore(name))
        tail_set, w_in, normed = sem("tail_set"), sem("w_in"), sem("normed")
        x_in = [sem(f"x_in{k}") for k in range(LOADS + 1)]
        sdve, h_ready, hT_ps, hT_ready, q_ps, kv_ps = sem("fdve"), sem("h_ready"), sem("hT_ps"), sem("hT_ready"), sem("q_ps"), sem("kv_ps")
        q_ready, kv_ready, h_out, acc_clear = sem("q_ready"), sem("kv_ready"), [sem("h_out0"), sem("h_out1")], sem("acc_clear")
        kv_out = [sem("kv_out0"), sem("kv_out1")]
        var_ready, std_ready, norm_ready = sem("var_ready"), sem("std_ready"), sem("norm_ready")
        block = ctx.enter_context(nc.Block())

        def tiles(eng, body):
            body(0, 0, 0)
            body(1, 1, 0)
            with eng.Fori(1, (NT - 1) // 2) as i:
                body(2 * i, 0, i)
                body(2 * i + 1, 1, i)
            body(NT - 1, 0, (NT - 1) // 2)

        @block.sync
        def _(sp):
            for k in range(LOADS):
                sp.dma_start(X[:, k * PER:(k + 1) * PER, :],
                             T.x[k * PER * P:(k + 1) * PER * P, :].rearrange("(t p) f -> p t f", p=P)).then_inc(x_in[k], 16)
            sp.wait_ge(tail_set, 1)
            sp.dma_start(X[0:TAIL, NT - 1, :], T.x[(NT - 1) * P:N, :]).then_inc(x_in[LOADS], 16)
            for j, w in enumerate((T.Wq, T.Wk, T.Wv)):
                sp.dma_start(wall[:, :, j * F:(j + 1) * F], w.rearrange("(k p) n -> p k n", p=P)).then_inc(w_in, 16)

            def body(t, b, turn):
                sp.wait_ge(h_ready, t + 1)
                sp.dma_start(T.h_tab[bass.ds(t * P, P), :], hs[:, b, :]).then_inc(h_out[b], 16)
                sp.wait_ge(kv_ready, t + 1)
                rows = T.kv_tab[bass.ds(t * P, P), :]
                sp.dma_start(rows, kv[:, b, :]).then_inc(kv_out[b], 16)
            tiles(sp, body)
            for stored in (h_out, kv_out):
                sp.wait_ge(stored[0], 16 * (NT // 2 + 1))
                sp.wait_ge(stored[1], 16 * (NT // 2))

        @block.vector
        def _(v):
            done = [0]

            def link(ins):
                done[0] += 1
                ins.then_inc(sdve, 1)
                v.wait_ge(sdve, done[0])
            nc.vector.memset(X[:, NT - 1, :], 0.0).then_inc(tail_set, 1)
            for k in range(LOADS):
                v.wait_ge(x_in[k], 16)
                with v.Fori(k * PER, (k + 1) * PER) as t:
                    nc.vector.bn_stats(stats[:, bass.ds(t, 1), :].rearrange("p a b -> p (a b)"),
                                       X[:, bass.ds(t, 1), :].rearrange("p a b -> p (a b)")).then_inc(normed, 1)
            v.wait_ge(x_in[LOADS], 16)
            nc.vector.bn_stats(stats[:, NT - 1, :], X[:, NT - 1, :]).then_inc(normed, 1)
            v.wait_ge(normed, NT)
            me, mo, se, so = (stats[:, :, j] for j in (1, 4, 2, 5))
            link(nc.vector.tensor_tensor(mean[:, :], me, mo, ALU.add))
            link(nc.vector.tensor_scalar(mean[:, :], mean[:, :], 0.5, None, ALU.mult))
            link(nc.vector.tensor_tensor(half[:, :], me, mean[:, :], ALU.subtract))
            link(nc.vector.tensor_tensor(half[:, :], half[:, :], half[:, :], ALU.mult))
            link(nc.vector.tensor_tensor(var[:, :], se, so, ALU.add))
            link(nc.vector.scalar_tensor_tensor(var[:, :], var[:, :], 1.0 / F, half[:, :], ALU.mult, ALU.add))
            nc.vector.tensor_scalar(var[:, :], var[:, :], EPS, None, ALU.add).then_inc(var_ready, 1)
            v.wait_ge(std_ready, 1)
            link(nc.vector.reciprocal(rstd[:, :], std[:, :]))
            nc.vector.scalar_tensor_tensor(nmr[:, :], mean[:, :], -1.0, rstd[:, :], ALU.mult, ALU.mult).then_inc(norm_ready, 1)

            def body(t, b, turn):
                v.wait_ge(hT_ps, t + 1)
                wait(v, q_ps, t - 1)
                wait(v, kv_ps, t - 1)
                nc.vector.tensor_copy(hT[:, b, :], ps[:, b, 0:F]).then_inc(hT_ready, 1)
                v.wait_ge(kv_ps, t + 1)
                wait(v, kv_out[b], 16 * turn)
                nc.vector.tensor_copy(kv[:, b, :], ps[:, 4 + b, :]).then_inc(kv_ready, 1)
            tiles(v, body)
            v.wait_ge(h_ready, NT)
            nc.vector.memset(c.acc[:, :], 0.0).then_inc(acc_clear, 1)

        @block.scalar
        def _(act):
            act.wait_ge(var_ready, 1)
            nc.scalar.activation(std[:, :], var[:, :], ACT.Sqrt).then_inc(std_ready, 1)
            act.wait_ge(norm_ready, 1)

            def body(t, b, turn):
                wait(act, hT_ps, t - 1)
                wait(act, h_out[b], 16 * turn)
                nc.scalar.activation(hs[:, b, :], X[:, bass.ds(t, 1), :].rearrange("p a b -> p (a b)"), ACT.Relu,
                                     bias=nmr[:, bass.ds(t, 1)], scale=rstd[:, bass.ds(t, 1)]).then_inc(h_ready, 1)
                act.wait_ge(q_ps, t + 1)
                nc.scalar.activation(c.q[:, bass.ds(t, 1), :].rearrange("p a b -> p (a b)"), ps[:, 2 + b, 0:F],
                                     ACT.Copy, scale=SCALE).then_inc(q_ready, 1)
            tiles(act, body)

        @block.tensor
        def _(pe):
            pe.wait_ge(w_in, 48)

            def body(t, b, turn):
                pe.wait_ge(h_ready, t + 1)
                wait(pe, hT_ready, t - 1)
                for k in range(2):
                    m = nc.tensor.transpose(ps[:, b, k * P:(k + 1) * P],
                                            hs[:, b, k * P:(k + 1) * P], c.ident[:, :])
                m.then_inc(hT_ps, 1)
                pe.wait_ge(hT_ready, t + 1)
                wait(pe, q_ready, t - 1)
                for k in range(2):
                    m = nc.tensor.matmul(ps[:, 2 + b, 0:F], hT[:, b, k * P:(k + 1) * P], wall[:, k, 0:F], start=(k == 0), stop=(k == 1))
                m.then_inc(q_ps, 1)
                wait(pe, kv_ready, t - 1)
                for k in range(2):
                    m = nc.tensor.matmul(ps[:, 4 + b, :], hT[:, b, k * P:(k + 1) * P], wall[:, k, F:3 * F], start=(k == 0), stop=(k == 1))
                m.then_inc(kv_ps, 1)
            tiles(pe, body)


def edge_phase(nc, T):
    c = T.c
    at = c.base + NTE * F

    def take(shape, dt=fp32):
        nonlocal at
        size = 1
        for n in shape[1:]:
            size *= n
        at += size
        return carve(T.arena, at - size, shape, dt)
    kv = take([P, U, G * 2 * F]).rearrange("p u (g f) -> p u g f", g=G)
    nodes = carve(T.arena, at, [P, U, EG // 2]).rearrange("p u f -> p (u f)").bitcast(i16).rearrange("p (u f) -> p u f", u=U)
    at += U * EG // 2
    hot_w = take([P, U, EG])
    hot_e = take([P, U, EG]).rearrange("p u (g w) -> p u g w", g=G)
    meta = take([P, U, 3 * G])
    flags = take([16, U, P])
    prod = take([P, G, F])
    pv = take([P, U, G * H * W]).rearrange("p u (g h w) -> p u g h w", g=G, h=H)
    score = take([P, 2, G * H])
    runmax = take([16, P])
    ends = take([P, G, H + 1])
    absent = take([P, G])
    local = take([P, G])
    grpmax = take([P, G, H])
    topmax = take([P, H])
    newmax = take([P, 2, H])
    fall = take([P, H])
    shift = take([P, G * H])
    decay = take([P, U, H])
    assert at <= 52600, at
    ps = T.psum
    qe = [ps[:, 2 * b:2 * b + 2, :].rearrange("p b (g f) -> p (b g) f", f=F) for b in range(2)]
    sums = [ps[:, 4 + b, 0:H * W] for b in range(2)]
    scoreT = ps[0:16, 6, 0:P]
    endsT = ps[:, 6, P:P + 16]
    grp = ps[:, 7, 0:G * (H + 1)].rearrange("p (g k) -> p g k", g=G)
    ref = ps[:, 7, 64:64 + G * H]
    acc = c.acc.rearrange("p (t h w) -> p t h w", h=H, w=W)
    LAST = NS + 4

    with ExitStack() as ctx:
        def sem(name):
            return ctx.enter_context(nc.semaphore(name))
        meta_in = [sem(f"meta_in{u}") for u in range(U)]
        rows_in = [sem(f"rows_in{u}") for u in range(U)]
        kv_in = [sem(f"kv_in{u}") for u in range(U)]
        hot_w_ready, hot_e_ready, ends_ready, prod_ready = sem("hot_w_ready"), sem("hot_e_ready"), sem("ends_ready"), sem("prod_ready")
        max_link, max_ready, score_ready, shift_ready = sem("max_link"), sem("max_ready"), sem("score_ready"), sem("shift_ready")
        local_ready = sem("local_ready")
        gather_begins, turn_begins = sem("gather_begins"), sem("turn_begins")
        scan_ready, added = sem("scan_ready"), sem("added")
        qe_ready, grp_ready, ref_ready, scoreT_ready, endsT_ready, sums_ready = (
            sem(n) for n in ("qe_ready", "grp_ready", "ref_ready", "scoreT_ready", "endsT_ready", "sums_ready"))
        p_ready, decay_ready, pv_ready, top_set = sem("p_ready"), sem("decay_ready"), sem("pv_ready"), sem("top_set")
        block = ctx.enter_context(nc.Block())

        def loop(eng, total, body, before=None):
            whole = total // U
            for i in range(U):
                body(i, i, 0, before(eng, i) if before and i == 0 else None)
            with eng.Fori(1, whole - 1) as k:
                for u in range(U):
                    body(U * k + u, u, k, before(eng, U * k) if before and u == 0 else None)
            for i in range((whole - 1) * U, total):
                body(i, i % U, i // U, None)

        def load(eng, row, s):
            return eng.value_load(row[0:1, bass.ds(s, 1)] if not isinstance(s, int) else row[0:1, s:s + 1],
                                  min_val=0, max_val=NG - 1 if row is c.ea_row else NT - 1)

        @block.sync
        def _(sp):
            def body(s, u, turn, _):
                ea = load(sp, c.ea_row, s)
                wait(sp, ends_ready, s - U + 1)
                sp.dma_start(meta[:, u, :], T.meta_tab[:, bass.ds(ea * (3 * G), 3 * G)]).then_inc(meta_in[u], 16)
                wait(sp, hot_w_ready, s - U + 1)
                sp.dma_start(nodes[:, u, :], T.dst_pad[bass.ds(ea * EG, EG)].partition_broadcast(P)).then_inc(rows_in[u], 16)
                wait(sp, scan_ready, s - U + 1)
                for g in range(1):
                    fl = T.flag_tab[bass.ds(ea * G, G), :].unsqueeze(1).broadcast_to([G, H, P])
                    sp.dma_start(flags[:, u, :], fl).then_inc(rows_in[u], 16)
            loop(sp, NS, body)

        @block.gpsimd
        def _(pool):
            def body(s, u, turn, _):
                pool.wait_ge(meta_in[u], 16 * (turn + 1))
                wait(pool, pv_ready, s - U + 1)
                pool.sem_inc(gather_begins, 1)
                for g in range(G):
                    pool.indirect_dma_start(out=kv[:, u, g, :], out_offset=None, in_=T.kv_tab[:, :],
                                            in_offset=bass.IndirectOffsetOnAxis(ap=meta[:, u, g:g + 1].bitcast(i32), axis=0),
                                            ).then_inc(kv_in[u], 16)
            loop(pool, NS, body)

        @block.vector
        def _(v):
            links = 4

            def build_hot_w(s, u, turn):
                v.wait_ge(rows_in[u], 32 * (turn + 1))
                wait(v, ref_ready, s - U + 1)
                nc.vector.tensor_scalar(hot_w[:, u, :], nodes[:, u, :],
                                        c.win_nodes[:, bass.ds(s, 1)], None, ALU.is_equal).then_inc(hot_w_ready, 1)

            nc.vector.memset(newmax[:, :, :], -BIG).then_inc(top_set, 1)
            def body(i, u, turn, _):
                one = isinstance(i, int)
                u1, t1 = (u - 1) % U, turn - (1 if u < 1 else 0)
                if one and i == 0:
                    for s in range(2):
                        build_hot_w(s, s, 0)
                if not one or 1 <= i <= NS:
                    v.wait_ge(endsT_ready, i)
                    wait(v, grp_ready, i - 1)
                    nc.vector.tensor_tensor(ends[:, :, 0:H], endsT.rearrange("p (g h) -> p g h", g=G),
                                            bcast(meta[:, u1, 2 * G:3 * G].unsqueeze(2), 2, H), ALU.mult)
                    nc.vector.tensor_scalar(ends[:, :, H:H + 1], meta[:, u1, 2 * G:3 * G].unsqueeze(2), BIG, None, ALU.mult).then_inc(ends_ready, 1)
                if not one or i < NS:
                    v.wait_ge(qe_ready, i + 1)
                    v.wait_ge(kv_in[u], 64 * (turn + 1))
                    wait(v, score_ready, i)
                    nc.vector.tensor_tensor(prod[:, :, :], kv[:, u, :, 0:F], qe[u % 2], ALU.mult).then_inc(prod_ready, 1)
                window = load(v, c.nt_row, i - 4) if not one or i >= 4 else None
                fresh, flush = not one or 1 <= i <= NS, not one or i >= 4
                if flush:
                    v.wait_ge(sums_ready, i - 3)
                    v.wait_ge(decay_ready, i - 3)
                    wait(v, added, i - 4)

                def add_head(h):
                    if flush:
                        a = acc[:, bass.ds(window, 1), h, :].rearrange("p a w -> p (a w)")
                        m = nc.vector.scalar_tensor_tensor(a, a, decay[:, u, h:h + 1], sums[u % 2][:, h * W:(h + 1) * W], ALU.mult, ALU.add)
                        if h == H - 1:
                            m.then_inc(added, 1)
                if fresh:
                    v.wait_ge(grp_ready, i)
                    n0 = links * (i - 1)
                    nc.vector.tensor_scalar(absent[:, :], grp[:, :, H], BIG, None, ALU.subtract).then_inc(max_link, 1)
                add_head(0)
                if fresh:
                    v.wait_ge(max_link, n0 + 1)
                    nc.vector.tensor_tensor(grpmax[:, :, :], grp[:, :, 0:H], bcast(absent[:, :].unsqueeze(2), 2, H), ALU.add).then_inc(max_link, 1)
                add_head(1)
                if fresh:
                    v.wait_ge(max_link, n0 + 2)
                    nc.vector.tensor_reduce(topmax[:, :], grpmax[:, :, :].rearrange("p g h -> p h g"), AX, ALU.max).then_inc(max_link, 1)
                add_head(2)
                if fresh:
                    v.wait_ge(max_link, n0 + 3)
                    wait(v, ref_ready, i - 2)
                    now, before = newmax[:, (u + 1) % 2, :], newmax[:, u % 2, :]
                    new = c.win_new[:, bass.ds(i - 1, 1)]
                    nc.vector.scalar_tensor_tensor(now, before, new, topmax[:, :], ALU.add, ALU.max).then_inc(max_link, 1)
                add_head(3)
                if fresh:
                    v.wait_ge(max_link, n0 + 4)
                    wait(v, decay_ready, i - 1)
                    nc.vector.scalar_tensor_tensor(fall[:, :], before, new, now, ALU.add, ALU.subtract).then_inc(max_ready, 1)
                if not one or i < NS:
                    nc.vector.tensor_scalar(local[:, :], meta[:, u, G:2 * G], c.win_base[:, bass.ds(i, 1)], None, ALU.subtract).then_inc(local_ready, 1)
                    v.wait_ge(prod_ready, i + 1)
                    nc.vector.tensor_reduce(score[:, u % 2, :], prod[:, :, :].rearrange("p g (h d) -> p (g h) d", h=H), AX, ALU.add).then_inc(score_ready, 1)
                if not one or 1 <= i <= NS:
                    v.wait_ge(ref_ready, i)
                    wait(v, p_ready, i - 1)
                    nc.vector.tensor_tensor(shift[:, :], score[:, (u + 1) % 2, :], ref, ALU.subtract).then_inc(shift_ready, 1)
                if not one or i < NS:
                    wait(v, sums_ready, i - U + 1)
                    v.wait_ge(local_ready, i + 1)
                    nc.vector.tensor_tensor(hot_e[:, u, :, :], bcast(c.iota[:, 0:P].unsqueeze(1), 1, G),
                                            bcast(local[:, :].unsqueeze(2), 2, P), ALU.is_equal).then_inc(hot_e_ready, 1)
                    v.wait_ge(scoreT_ready, i + 1)
                    wait(v, endsT_ready, i)
                    nc.vector.tensor_tensor_scan(runmax[:, :], flags[:, u, :], scoreT, -BIG, ALU.add, ALU.max).then_inc(scan_ready, 1)
                if not one or i + 2 < NS:
                    build_hot_w(i + 2, (u + 2) % U, turn + (1 if u >= 2 else 0))
            v.wait_ge(top_set, 1)
            loop(v, LAST, body)

        @block.scalar
        def _(act):
            def body(s, u, turn, _):
                act.wait_ge(shift_ready, s + 1)
                wait(act, sums_ready, s - U + 1)
                nc.scalar.activation(pv[:, u, :, :, D:W].rearrange("p g h w -> p (g h w)"), shift[:, :], ACT.Exp).then_inc(p_ready, 1)
                act.wait_ge(max_ready, s + 1)
                wait(act, added, s - U + 1)
                nc.scalar.activation(decay[:, u, :], fall[:, :], ACT.Exp).then_inc(decay_ready, 1)
                act.wait_ge(p_ready, s + 1)
                for g in range(G):
                    for h in range(H):
                        m = nc.scalar.activation(pv[:, u, g, h, 0:D], kv[:, u, g, F + h * D:F + (h + 1) * D], ACT.Copy,
                                                 scale=pv[:, u, g, h, D:W])
                m.then_inc(pv_ready, 1)
            loop(act, NS, body)

        @block.tensor
        def _(pe):
            nts = {}

            def queries(s, u, window):
                pe.wait_ge(hot_w_ready, s + 1)
                wait(pe, prod_ready, s - 1)
                qw = c.q[:, bass.ds(window, 1), :].rearrange("p a f -> p (a f)")
                for g in range(G):
                    m = nc.tensor.matmul(qe[u % 2][:, g, :], hot_w[:, u, g * P:(g + 1) * P], qw, start=True, stop=True)
                m.then_inc(qe_ready, 1)

            def body(i, u, turn, _):
                one = isinstance(i, int)
                u1, u3 = (u - 1) % U, (u - 3) % U
                if one and i == 0:
                    queries(0, 0, load(pe, c.nt_row, 0))
                if not one or 1 <= i <= NS:
                    pe.wait_ge(ends_ready, i)
                    pe.wait_ge(hot_e_ready, i)
                    wait(pe, max_ready, i - 1)
                    for g in range(G):
                        m = nc.tensor.matmul(grp[:, g, :], hot_e[:, u1, g, :], ends[:, g, :], start=True, stop=True)
                    m.then_inc(grp_ready, 1)
                if not one or i + 1 < NS:
                    queries(i + 1, (u + 1) % U, load(pe, c.nt_row, i + 1))
                if not one or 1 <= i <= NS:
                    pe.wait_ge(max_ready, i)
                    wait(pe, shift_ready, i - 1)
                    for g in range(G):
                        m = nc.tensor.matmul(ref[:, g * H:(g + 1) * H], hot_w[:, u1, g * P:(g + 1) * P], newmax[:, (u + 1) % 2, :], start=True, stop=True)
                    m.then_inc(ref_ready, 1)
                if not one or i < NS:
                    pe.wait_ge(score_ready, i + 1)
                    wait(pe, scan_ready, i)
                    nc.tensor.transpose(scoreT, score[:, u % 2, :], c.ident[:, :]).then_inc(scoreT_ready, 1)
                def sum_tiles(tiles):
                    for g in tiles:
                        m = nc.tensor.matmul(sums[(u + 1) % 2], hot_e[:, u3, g, :], pv[:, u3, g, :, :].rearrange("p h w -> p (h w)"),
                                             start=(g == 0), stop=(g == G - 1))
                        if g == G - 1:
                            m.then_inc(sums_ready, 1)
                due = not one or 3 <= i < NS + 3
                if due:
                    pe.wait_ge(pv_ready, i - 2)
                    wait(pe, added, i - 4)
                    sum_tiles(range(0, G // 2))
                if not one or i < NS:
                    pe.wait_ge(scan_ready, i + 1)
                    wait(pe, ends_ready, i)
                    pe.sem_inc(turn_begins, 1)
                    nc.tensor.transpose(endsT, runmax[:, :], c.ident[0:16, 0:16]).then_inc(endsT_ready, 1)
                if due:
                    sum_tiles(range(G // 2, G))
            loop(pe, LAST, body)


def node_phase(nc, T):
    c = T.c
    at = c.base

    def take(shape, dt=fp32):
        nonlocal at
        size = 1
        for n in shape[1:]:
            size *= n
        at += size
        return carve(T.arena, at - size, shape, dt)
    KF, KH = F // P, HID // P
    w1 = take([P, KF, HID])
    w2 = take([P, KH, F])
    wx = take([P, KF, F + 2 * H])
    att = take([P, 2, F])
    attw = take([P, F])
    gain, shift, b2 = take([P, F]), take([P, F]), take([P, F])
    b1, slope = take([P, KH]), take([P, KH])
    c.edge_src = take([P, NT], i32)
    c.edge_dst = take([P, NT], i32)
    rden = take([P, NT, H])
    hin, xin = take([P, 2, F]), take([P, 2, F])
    r = take([P, F])
    rst = take([P, 2, F])
    rstT = take([P, KF, P])
    hid = take([P, KH, P])
    above, below = take([P, KH, P]), take([P, KH, P])
    b1n = take([P, KH])
    y = take([P, F])
    z = take([P, F])
    h2T = take([P, KF, P])
    xt = take([P, 2, F + 2 * H])
    stA, stC, stD = take([P, 6]), take([P, 6]), take([P, 6])
    mvA, mvC, mvD = take([P, 2]), take([P, 2]), take([P, 2])
    sdA, sdC, sdD = take([P, 1]), take([P, 1]), take([P, 1])
    assert at <= 52600, at
    ps = T.psum
    rstT_ps, h2T_ps = ps[:, 0, 0:F], ps[:, 4, 0:F]
    hid_ps = ps[:, 1:3, :].rearrange("p b (k n) -> p (b k) n", n=P)
    ffn_ps, xt_ps = ps[:, 3, 0:F], ps[:, 5, 0:F + 2 * H]
    acc4 = c.acc.rearrange("p (t h w) -> p t h w", h=H, w=W)
    accF = c.acc.rearrange("p (t f) -> p t f", f=H * W)
    LINKS_A, LINKS_C, LINKS_D = 7, 8, 3

    def tile_of(view, t):
        return view[:, bass.ds(t, 1), :].rearrange("p a f -> p (a f)")

    with ExitStack() as ctx:
        def sem(name):
            return ctx.enter_context(nc.semaphore(name))
        w_in, idx_in, x_clear, setup, den_ready = sem("w_in"), sem("idx_in"), sem("x_clear"), sem("setup"), sem("den_ready")
        h_in, x_in = [sem("h_in0"), sem("h_in1")], [sem("x_in0"), sem("x_in1")]
        xt_out = [sem("xt_out0"), sem("xt_out1")]
        chA, chC, chD = sem("chain_a"), sem("chain_c"), sem("chain_d")
        varA, varC, varD, sdA_ok, sdC_ok, sdD_ok = (sem(n) for n in ("var_a", "var_c", "var_d", "std_a", "std_c", "std_d"))
        rst_ready, rstT_done, x2_ready, h2_ready, h2T_ready = (sem(n) for n in ("rst_ready", "rstT_done", "x2_ready", "h2_ready", "h2T_ready"))
        rstT_mm, hid_mm, ffn_mm, h2T_mm, xt_mm, hid_ready, xt_ready = (
            sem(n) for n in ("rstT_mm", "hid_mm", "ffn_mm", "h2T_mm", "xt_mm", "hid_ready", "xt_ready"))
        stats_begun = sem("stats_begun")
        halves = sem("halves")
        h_used, x_used = sem("h_used"), sem("x_used")
        block = ctx.enter_context(nc.Block())

        def loop(eng, body):
            body(0, 0, 0)
            body(1, 1, 0)
            with eng.Fori(1, (NT - 3) // 2) as k:
                body(2 * k, 0, k)
                body(2 * k + 1, 1, k)
            for i in range(NT - 3, NT + 1):
                body(i, i % 2, i // 2)

        def inner(i, lo, hi):
            return not isinstance(i, int) or lo <= i < hi

        @block.sync
        def _(sp):
            for tile, src in ((w1, T.W1.rearrange("(k p) n -> p k n", p=P)), (w2, T.W2.rearrange("(k p) n -> p k n", p=P)),
                              (wx[:, :, 0:F], T.weight.rearrange("(k p) n -> p k n", p=P)),
                              (att[:, 0, :], T.attn_r.rearrange("h d -> (h d)").partition_broadcast(P)),
                              (att[:, 1, :], T.attn_l.rearrange("h d -> (h d)").partition_broadcast(P)),
                              (gain, T.ln_g.partition_broadcast(P)), (shift, T.ln_b.partition_broadcast(P)), (b2, T.b2.partition_broadcast(P)),
                              (b1, T.b1.rearrange("(k p) -> p k", p=P)), (slope, T.alpha.rearrange("(k p) -> p k", p=P))):
                sp.dma_start(tile, src, allow_slow_non_contiguous=True).then_inc(w_in, 16)

            def load_h(t, b):
                sp.dma_start(hin[:, b, :], T.h_tab[bass.ds(t * P, P), :]).then_inc(h_in[b], 16)

            def load_x(t, b):
                if isinstance(t, int) and t == NT - 1:
                    sp.dma_start(xin[0:TAIL, b, :], T.x[t * P:N, :]).then_inc(x_in[b], 16)
                else:
                    sp.dma_start(xin[:, b, :], T.x[bass.ds(t * P, P), :]).then_inc(x_in[b], 16)
            load_h(0, 0)
            load_h(1, 1)
            sp.dma_start(c.edge_src, T.src[0:NT * P].rearrange("(t p) -> p t", p=P), allow_slow_non_contiguous=True).then_inc(idx_in, 16)
            sp.dma_start(c.edge_dst, T.dst[0:NT * P].rearrange("(t p) -> p t", p=P), allow_slow_non_contiguous=True).then_inc(idx_in, 16)

            def body(i, b, turn):
                if inner(i, 0, NT - 2):
                    sp.wait_ge(h_used, i + 1)
                    load_h(i + 2, b)
                if inner(i, 0, NT):
                    sp.wait_ge(x_clear, 1)
                    wait(sp, x_used, i - 1)
                    load_x(i, b)
                if inner(i, 2, NT + 1):
                    sp.wait_ge(xt_ready, i - 1)
                    store(i - 2, b)

            def store(t, b):
                sp.dma_start(T.xt_tab[bass.ds(t * P, P), :], xt[:, b, 0:F + H]).then_inc(xt_out[b], 16)
                sp.dma_start(T.al_tab[bass.ds(t * P, P), :], xt[:, b, F + H:F + 2 * H]).then_inc(xt_out[b], 16)
            loop(sp, body)
            sp.wait_ge(xt_ready, NT)
            store(NT - 1, 0)
            sp.wait_ge(idx_in, 32)
            sp.wait_ge(xt_out[0], 32 * (NT // 2 + 1))
            sp.wait_ge(xt_out[1], 32 * (NT // 2))

        @block.vector
        def _(v):
            def chain(sem_, per, t):
                k = [0]

                def link(ins):
                    k[0] += 1
                    ins.then_inc(sem_, 1)
                    v.wait_ge(sem_, per * t + k[0])
                return link
            nc.vector.memset(xin[:, :, :], 0.0).then_inc(x_clear, 1)
            link = chain(setup, 0, 0)
            v.wait_ge(w_in, 16 * 10)
            for k in range(KF):
                for j in range(2):
                    link(nc.vector.tensor_tensor(attw, wx[:, k, 0:F], att[:, j, :], ALU.mult))
                    link(nc.vector.tensor_reduce(wx[:, k, F + j * H:F + (j + 1) * H], attw.rearrange("p (h d) -> p h d", h=H), AX, ALU.add))
            link(nc.vector.tensor_scalar(b1n, b1, -1.0, None, ALU.mult))
            link(nc.vector.tensor_scalar(slope, slope, -1.0, None, ALU.mult))
            link(nc.vector.tensor_scalar(rden, acc4[:, 0:NT, :, D], 1.0e-30, None, ALU.max))
            link(nc.vector.reciprocal(rden, rden))

            def stats(link, src, st, mv, var_sem):
                link(nc.vector.bn_stats(st, src))
                v.sem_inc(stats_begun, 1)
                link(nc.vector.bn_aggr(mv, st))
                nc.vector.tensor_scalar(mv[:, 1:2], mv[:, 1:2], EPS, None, ALU.add).then_inc(var_sem, 1)

            def first_a(t, b, turn):
                link = chain(chA, LINKS_A, t)
                a = acc4[:, bass.ds(t, 1), :, 0:D].rearrange("p a h d -> p (a h) d")
                rd = rden[:, bass.ds(t, 1), :].rearrange("p a h -> p (a h)").unsqueeze(2)
                link(nc.vector.tensor_tensor(r.rearrange("p (h d) -> p h d", h=H), a, bcast(rd, 2, D), ALU.mult))
                v.wait_ge(h_in[b], 16 * (turn + 1))
                ins = nc.vector.tensor_tensor(r, r, hin[:, b, :], ALU.add)
                link(ins)
                v.sem_inc(h_used, 1)
                stats(link, r, stA, mvA, varA)
                return link

            def second_a(link, t, b):
                v.wait_ge(sdA_ok, t + 1)
                link(nc.vector.reciprocal(sdA, sdA))
                link(nc.vector.tensor_scalar(r, r, mvA[:, 0:1], sdA[:, 0:1], ALU.subtract, ALU.mult))
                link(nc.vector.tensor_tensor(r, r, gain, ALU.mult))
                wait(v, rstT_mm, t - 1)
                nc.vector.tensor_tensor(rst[:, b, :], r, shift, ALU.add).then_inc(rst_ready, 1)

            def first_c(t, b):
                link = chain(chC, LINKS_C, t)
                v.wait_ge(ffn_mm, t + 1)
                link(nc.vector.tensor_tensor(y, ffn_ps, rst[:, b, :], ALU.add))
                link(nc.vector.tensor_tensor(y, y, b2, ALU.add))
                stats(link, y, stC, mvC, varC)
                return link

            def second_c(link, t, b, turn):
                v.wait_ge(sdC_ok, t + 1)
                link(nc.vector.reciprocal(sdC, sdC))
                link(nc.vector.tensor_scalar(y, y, mvC[:, 0:1], sdC[:, 0:1], ALU.subtract, ALU.mult))
                link(nc.vector.tensor_tensor(y, y, gain, ALU.mult))
                link(nc.vector.tensor_tensor(y, y, shift, ALU.add))
                v.wait_ge(x_in[b], 16 * (turn + 1))
                x2 = accF[:, bass.ds(t, 1), 0:F].rearrange("p a f -> p (a f)")
                nc.vector.tensor_tensor(x2, y, xin[:, b, :], ALU.add).then_inc(x2_ready, 1)
                v.wait_ge(x2_ready, t + 1)
                v.sem_inc(x_used, 1)
                link = chain(chD, LINKS_D, t)
                stats(link, x2, stD, mvD, varD)
                return link

            def last_c(link, t, b):
                v.wait_ge(sdD_ok, t + 1)
                link(nc.vector.reciprocal(sdD, sdD))
                wait(v, h2T_mm, t)
                x2 = accF[:, bass.ds(t, 1), 0:F].rearrange("p a f -> p (a f)")
                nc.vector.tensor_scalar(z, x2, mvD[:, 0:1], sdD[:, 0:1], ALU.subtract, ALU.mult).then_inc(h2_ready, 1)

            link = first_a(0, 0, 0)
            second_a(link, 0, 0)

            def body(i, b, turn):
                b1_, t1 = 1 - b, turn - (1 - b)
                if inner(i, 0, NT):
                    v.wait_ge(rstT_mm, i + 1)
                    wait(v, hid_mm, 2 * i)
                    nc.vector.tensor_copy(rstT.rearrange("p k n -> p (k n)"), rstT_ps).then_inc(rstT_done, 1)
                if inner(i, 0, NT - 1):
                    la = first_a(i + 1, b1_, turn + b)
                if inner(i, 1, NT + 1):
                    lc = first_c(i - 1, b1_)
                if inner(i, 0, NT - 1):
                    second_a(la, i + 1, b1_)
                if inner(i, 0, NT):
                    wait(v, ffn_mm, i)
                    for k in range(KH):
                        v.wait_ge(halves, KH * i + k + 1)
                        nc.vector.scalar_tensor_tensor(hid[:, k, :], below[:, k, :], slope[:, k:k + 1], above[:, k, :],
                                                       ALU.mult, ALU.add).then_inc(hid_ready, 1)
                if inner(i, 1, NT + 1):
                    ld = second_c(lc, i - 1, b1_, t1)
                    last_c(ld, i - 1, b1_)
            loop(v, body)

        @block.scalar
        def _(act):
            def root(var_sem, mv, sd, ok, t):
                act.wait_ge(var_sem, t + 1)
                nc.scalar.activation(sd, mv[:, 1:2], ACT.Sqrt).then_inc(ok, 1)
            root(varA, mvA, sdA, sdA_ok, 0)
            act.wait_ge(setup, 4 * KF + 1)

            def body(i, b, turn):
                if inner(i, 0, NT - 1):
                    root(varA, mvA, sdA, sdA_ok, i + 1)
                if inner(i, 1, NT + 1):
                    root(varC, mvC, sdC, sdC_ok, i - 1)
                if inner(i, 0, NT):
                    for k in range(KH):
                        act.wait_ge(hid_mm, 2 * i + 1 + k // (KH // 2))
                        if k == 0:
                            wait(act, hid_ready, KH * i)
                        nc.scalar.activation(above[:, k, :], hid_ps[:, k, :], ACT.Relu, bias=b1[:, k:k + 1])
                        nc.scalar.activation(below[:, k, :], hid_ps[:, k, :], ACT.Relu, bias=b1n[:, k:k + 1], scale=-1.0).then_inc(halves, 1)
                if inner(i, 1, NT + 1):
                    root(varD, mvD, sdD, sdD_ok, i - 1)
                    act.wait_ge(h2T_mm, i)
                    wait(act, xt_mm, i - 1)
                    nc.scalar.activation(h2T.rearrange("p k n -> p (k n)"), h2T_ps, ACT.Relu).then_inc(h2T_ready, 1)
                    act.wait_ge(xt_mm, i)
                    wait(act, xt_out[1 - b], 32 * (turn - (1 - b)))
                    nc.scalar.copy(xt[:, 1 - b, :], xt_ps).then_inc(xt_ready, 1)
            loop(act, body)

        @block.tensor
        def _(pe):
            def body(i, b, turn):
                if inner(i, 0, NT):
                    pe.wait_ge(rst_ready, i + 1)
                    wait(pe, rstT_done, i)
                    for k in range(KF):
                        m = nc.tensor.transpose(rstT_ps[:, k * P:(k + 1) * P], rst[:, b, k * P:(k + 1) * P], c.ident)
                    m.then_inc(rstT_mm, 1)
                    pe.wait_ge(rstT_done, i + 1)
                    for n in range(KH):
                        if n % (KH // 2) == 0:
                            wait(pe, halves, KH * (i - 1) + n + KH // 2)
                        for k in range(KF):
                            m = nc.tensor.matmul(hid_ps[:, n, :], w1[:, k, n * P:(n + 1) * P], rstT[:, k, :], start=(k == 0), stop=(k == KF - 1))
                        if n % (KH // 2) == KH // 2 - 1:
                            m.then_inc(hid_mm, 1)
                if inner(i, 1, NT + 1):
                    wait(pe, x2_ready, i)
                if inner(i, 0, NT):
                    for n in range(KH):
                        pe.wait_ge(hid_ready, KH * i + n + 1)
                        m = nc.tensor.matmul(ffn_ps, hid[:, n, :], w2[:, n, :], start=(n == 0), stop=(n == KH - 1))
                    m.then_inc(ffn_mm, 1)
                if inner(i, 1, NT + 1):
                    pe.wait_ge(h2_ready, i)
                    wait(pe, h2T_ready, i - 1)
                    for k in range(KF):
                        m = nc.tensor.transpose(h2T_ps[:, k * P:(k + 1) * P], z[:, k * P:(k + 1) * P], c.ident)
                    m.then_inc(h2T_mm, 1)
                    pe.wait_ge(h2T_ready, i)
                    wait(pe, xt_ready, i - 1)
                    for k in range(KF):
                        m = nc.tensor.matmul(xt_ps, h2T[:, k, :], wx[:, k, :], start=(k == 0), stop=(k == KF - 1))
                    m.then_inc(xt_mm, 1)
            pe.wait_ge(setup, 4 * KF)
            loop(pe, body)


def output_phase(nc, T):
    c = T.c
    at = c.base + 12000
    xg = carve(T.arena, at, [P, NT, F + H]); at += NT * (F + H)
    al = carve(T.arena, at, [P, NT, H]); at += NT * H
    sc = carve(T.arena, at, [P, NT, H]); at += NT * H
    mx = carve(T.arena, at, [P, NT]); at += NT
    mixed = carve(T.arena, at, [P, NT, D]); at += NT * D
    assert at <= 52600, at
    accF = c.acc.rearrange("p (t f) -> p t f", f=H * W)
    PER, LINKS = 7, 10
    PARTS = NT // PER
    with ExitStack() as ctx:
        def sem(name):
            return ctx.enter_context(nc.semaphore(name))
        rows_in = [sem(f"rows_in{k}") for k in range(PARTS)]
        link_sem, shifted, powered, part_ready, stored = sem("link"), sem("shifted"), sem("powered"), sem("part_ready"), sem("stored")
        block = ctx.enter_context(nc.Block())

        @block.gpsimd
        def _(pool):
            for t in range(NT):
                for tab, tile, ids in ((T.al_tab, al[:, t, :], c.edge_src), (T.xt_tab, xg[:, t, :], c.edge_dst)):
                    pool.indirect_dma_start(out=tile, out_offset=None, in_=tab[:, :],
                                            in_offset=bass.IndirectOffsetOnAxis(ap=ids[:, t:t + 1], axis=0)).then_inc(rows_in[t // PER], 16)

        @block.vector
        def _(v):
            done = [0]

            def link(ins):
                done[0] += 1
                ins.then_inc(link_sem, 1)
                v.wait_ge(link_sem, done[0])
            for k in range(PARTS):
                ts = slice(k * PER, (k + 1) * PER)
                s, m = sc[:, ts, :], mx[:, ts]
                v.wait_ge(rows_in[k], 32 * PER)
                link(nc.vector.tensor_tensor(s, al[:, ts, :], xg[:, ts, F:F + H], ALU.add))
                link(nc.vector.scalar_tensor_tensor(s, s, 0.01, s, ALU.mult, ALU.max))
                link(nc.vector.tensor_reduce(m, s, AX, ALU.max))
                nc.vector.tensor_tensor(s, s, bcast(m.unsqueeze(2), 2, H), ALU.subtract).then_inc(shifted, 1)
                v.wait_ge(powered, k + 1)
                link(nc.vector.tensor_reduce(m, s, AX, ALU.add))
                link(nc.vector.reciprocal(m, m))
                link(nc.vector.tensor_tensor(s, s, bcast(m.unsqueeze(2), 2, H), ALU.mult))
                heads = xg[:, ts, 0:F].rearrange("p t (h d) -> p t h d", h=H)
                link(nc.vector.tensor_tensor(heads, heads, bcast(s.unsqueeze(3), 3, D), ALU.mult))
                link(nc.vector.tensor_tensor(heads[:, :, 0:2, :], heads[:, :, 0:2, :], heads[:, :, 2:4, :], ALU.add))
                link(nc.vector.tensor_tensor(mixed[:, ts, :], heads[:, :, 0, :], heads[:, :, 1, :], ALU.add))
                o = accF[:, ts, 0:F].rearrange("p t (h d) -> p t h d", h=H)
                nc.vector.tensor_tensor(o, o, bcast(mixed[:, ts, :].unsqueeze(2), 2, H), ALU.add).then_inc(part_ready, 1)

        @block.scalar
        def _(act):
            for k in range(PARTS):
                s = sc[:, k * PER:(k + 1) * PER, :]
                act.wait_ge(shifted, k + 1)
                nc.scalar.activation(s, s, ACT.Exp).then_inc(powered, 1)

        @block.sync
        def _(sp):
            for k in range(PARTS):
                sp.wait_ge(part_ready, k + 1)
                whole = min((k + 1) * PER, NT - 1)
                sp.dma_start(T.out[k * PER * P:whole * P, :].rearrange("(t p) f -> p t f", p=P), accF[:, k * PER:whole, 0:F]).then_inc(stored, 16)
            sp.dma_start(T.out[(NT - 1) * P:N, :], accF[0:TAIL, NT - 1, 0:F]).then_inc(stored, 16)
            sp.wait_ge(stored, 16 * (PARTS + 1))


_INS = ['x', 'src', 'dst', 'L0_gnn_Wq', 'L0_gnn_Wk', 'L0_gnn_Wv', 'L0_gnn_ln_g', 'L0_gnn_ln_b', 'L0_gnn_W1', 'L0_gnn_b1',
        'L0_gnn_alpha', 'L0_gnn_W2', 'L0_gnn_b2', 'L1_gnn_weight', 'L1_gnn_attn_l', 'L1_gnn_attn_r']


def kernel(**inputs):
    import numpy as _np
    import concourse.bacc as _bacc
    from concourse import mybir as _mybir
    from concourse.bass_utils import run_bass_kernel_spmd as _run

    nc = _bacc.Bacc("TRN2", target_bir_lowering=False, num_devices=1)
    arrays, args = {}, []
    for name in _INS:
        a = _np.ascontiguousarray(inputs[name])
        arrays[f"in_{name}"] = a
        args.append(nc.dram_tensor(f"in_{name}", a.shape, _mybir.dt.from_np(a.dtype), kind="ExternalInput").ap())
    args.append(nc.dram_tensor("out_0", (N, F), fp32, kind="ExternalOutput").ap())
    gnn_kernel(nc, *args)
    r = _run(nc, [arrays], core_ids=[0])
    return r.results[0]["out_0"]
```

```python
import concourse.bass as bass
from concourse import mybir
from contextlib import ExitStack

fp32 = mybir.dt.float32
i32 = mybir.dt.int32
i16 = mybir.dt.int16
ALU = mybir.AluOpType
ACT = mybir.ActivationFunctionType
AX = mybir.AxisListType.X

P = 128
N, F = 6250, 256
H, D = 4, 64
HID = 4 * F
E = 200000
NT = -(-N // P)
TAIL = N - (NT - 1) * P
NTE = NT + 1
G = 4
EG = G * P
NG = -(-E // EG)
NROW = NG * G
NCH = -(-NROW // P)
NS = NG + NT - 1
W = D + 1
U = 4
BIG = 2.0 ** 100
PAD_DST = 8191
LOADS = 4
PER = (NT - 1) // LOADS
EPS = 1e-5
SCALE = 1.0 / 16.0


class Names:
    pass


def carve(arena, at, shape, dt=fp32):
    size = 1
    for n in shape[1:]:
        size *= n
    v = arena[0:shape[0], at:at + size]
    if dt is not fp32:
        v = v.bitcast(dt)
    if len(shape) == 3:
        v = v.rearrange("p (a b) -> p a b", b=shape[2])
    if len(shape) == 4:
        v = v.rearrange("p (a b c) -> p a b c", b=shape[2], c=shape[3])
    return v


def wait(eng, sem, value):
    if isinstance(value, int) and value <= 0:
        return
    eng.wait_ge(sem, value)


def bcast(ap, axis, n):
    shape = list(ap.shape)
    shape[axis] = n
    return ap.broadcast_to(shape)


def gnn_kernel(nc, x, src, dst, Wq, Wk, Wv, ln_g, ln_b, W1, b1, alpha, W2, b2, weight, attn_l, attn_r, out):
    kv_tab = nc.dram_tensor("kv_tab", (NT * P, 2 * F), fp32, kind="Internal").ap()
    h_tab = nc.dram_tensor("h_tab", (NT * P, F), fp32, kind="Internal").ap()
    xt_tab = nc.dram_tensor("xt_tab", (NT * P, F + H), fp32, kind="Internal").ap()
    al_tab = nc.dram_tensor("al_tab", (NT * P, H), fp32, kind="Internal").ap()
    dst_pad = nc.dram_tensor("dst_pad", (NROW * P,), i16, kind="Internal").ap()
    flag_tab = nc.dram_tensor("flag_tab", (NROW, P), fp32, kind="Internal").ap()
    meta_tab = nc.dram_tensor("meta_tab", (P, NG * 3 * G), fp32, kind="Internal").ap()
    T = Names()
    T.x, T.src, T.dst, T.out = x, src, dst, out
    T.Wq, T.Wk, T.Wv, T.ln_g, T.ln_b = Wq, Wk, Wv, ln_g, ln_b
    T.W1, T.b1, T.alpha, T.W2, T.b2 = W1, b1, alpha, W2, b2
    T.weight, T.attn_l, T.attn_r = weight, attn_l, attn_r
    T.kv_tab, T.h_tab, T.xt_tab, T.al_tab = kv_tab, h_tab, xt_tab, al_tab
    T.dst_pad, T.flag_tab, T.meta_tab = dst_pad, flag_tab, meta_tab
    with ExitStack() as ctx:
        T.arena = ctx.enter_context(nc.sbuf_tensor("arena", [P, 52600], fp32))
        T.psum = ctx.enter_context(nc.psum_tensor("psum", [P, 8, 512], fp32))
        c = Names()
        at = 0

        def keep(shape, dt=fp32):
            nonlocal at
            size = 1
            for n in shape[1:]:
                size *= n
            at += size
            return carve(T.arena, at - size, shape, dt)
        c.acc = keep([P, NTE * H * W])
        c.ident = keep([P, P])
        c.win_nodes = keep([P, NS])
        c.nt_row = keep([1, NS + 1], i32)
        c.ea_row = keep([1, NS + 1], i32)
        c.win_base = keep([P, NS])
        c.win_new = keep([P, NS])
        c.iota = keep([P, EG])
        c.stats = keep([P, NT * 6]).rearrange("p (t k) -> p t k", k=6)
        c.base = at
        T.c = c
        c.x_in = [ctx.enter_context(nc.semaphore(f"x_loaded{k}")) for k in range(LOADS + 1)]
        schedule_phase(nc, T)
        feature_phase(nc, T)
        edge_phase(nc, T)
        node_phase(nc, T)
        output_phase(nc, T)


def schedule_phase(nc, T):
    c = T.c
    at = c.base
    dst_i = carve(T.arena, at, [P, NCH, P], i32); at += NCH * P
    src_i = carve(T.arena, at, [P, NCH, P], i32); at += NCH * P
    dst_s = carve(T.arena, at, [P, NCH * P // 2]).bitcast(i16).rearrange("p (c f) -> p c f", f=P); at += NCH * P // 2
    dst_f = carve(T.arena, at, [P, NCH, P]); at += NCH * P
    src_f = carve(T.arena, at, [P, NCH, P]); at += NCH * P
    start = carve(T.arena, at, [P, NCH, P]); at += NCH * P
    end = carve(T.arena, at, [P, NCH, P]); at += NCH * P
    meta = carve(T.arena, at, [P, NCH * P // G, 3 * G]); at += NCH * P * 3
    meta_i = meta.bitcast(i32)
    last = carve(T.arena, at, [NT - 1, NG, 3 * G]); at += NG * 3 * G
    less = carve(T.arena, at, [NT - 1, NG]); at += NG
    iota_row = c.iota[:, 0:P]
    X = c.acc[:, 0:NT * F].rearrange("p (t f) -> p t f", f=F)
    part = carve(T.arena, at, [P, 1]); at += 1
    limit = carve(T.arena, at, [P, 1]); at += 1
    turn = carve(T.arena, at, [P, 1]); at += 1
    reach = carve(T.arena, at, [NT - 1, NS]); at += NS
    ones = carve(T.arena, at, [NT - 1, P]); at += P
    nt_f = carve(T.arena, at, [P, NS]); at += NS
    ea_f = carve(T.arena, at, [1, NS]); at += NS
    ps = T.psum
    full = E // P
    rows_last = NROW - (NCH - 1) * P
    full_last = full - (NCH - 1) * P
    rest = E - full * P
    with ExitStack() as ctx:
        def sem(name):
            return ctx.enter_context(nc.semaphore(name))
        shorts_set, tail_set, normed = sem("shorts_set"), sem("tail_set"), sem("normed")
        pads_set, edges_in, padded_out, iotas = sem("pads_set"), sem("edges_in"), sem("padded_out"), sem("iotas")
        dve, transposed, meta_built, meta_out, last_in = sem("sdve"), sem("transposed"), sem("meta_built"), sem("meta_out"), sem("last_in")
        consts, nt_counted, reached, flags_set, flags_out = sem("consts"), sem("nt_counted"), sem("reached"), sem("flags_set"), sem("flags_out")
        block = ctx.enter_context(nc.Block())

        @block.sync
        def _(sp):
            sp.wait_ge(pads_set, 2)
            for lst, tile in ((T.dst, dst_i), (T.src, src_i)):
                sp.dma_start(tile[:, 0:NCH - 1, :], lst[0:(NCH - 1) * P * P].rearrange("(c p f) -> p c f", p=P, f=P)).then_inc(edges_in, 16)
                sp.dma_start(tile[0:full_last, NCH - 1, :], lst[(NCH - 1) * P * P:full * P].rearrange("(p f) -> p f", f=P)).then_inc(edges_in, 16)
                sp.dma_start(tile[full_last:full_last + 1, NCH - 1, 0:rest], lst[full * P:E].unsqueeze(0)).then_inc(edges_in, 16)
            sp.wait_ge(shorts_set, 1)
            sp.dma_start(T.dst_pad[0:(NCH - 1) * P * P].rearrange("(c p f) -> p c f", p=P, f=P), dst_s[:, 0:NCH - 1, :]).then_inc(padded_out, 16)
            sp.dma_start(T.dst_pad[(NCH - 1) * P * P:NROW * P].rearrange("(p f) -> p f", f=P), dst_s[0:rows_last, NCH - 1, :]).then_inc(padded_out, 16)
            sp.wait_ge(flags_set, 1)
            sp.dma_start(T.flag_tab[0:(NCH - 1) * P, :].rearrange("(c p) f -> p c f", p=P), start[:, 0:NCH - 1, :]).then_inc(flags_out, 16)
            sp.dma_start(T.flag_tab[(NCH - 1) * P:NROW, :], start[0:rows_last, NCH - 1, :]).then_inc(flags_out, 16)
            sp.wait_ge(meta_built, 3 * NCH)
            sp.dma_start(T.meta_tab[:, :], meta[:, 0:NG, :].rearrange("p a b -> p (a b)")).then_inc(meta_out, 16)
            sp.wait_ge(meta_out, 16)
            sp.dma_start(last[:, :, :].rearrange("p a b -> p (a b)"), T.meta_tab[P - 1:P, :].broadcast_to([NT - 1, NG * 3 * G])).then_inc(last_in, 16)
            sp.wait_ge(padded_out, 32)
            sp.wait_ge(flags_out, 32)

        @block.scalar
        def _(act):
            act.wait_ge(tail_set, 1)
            act.dma_start(X[0:TAIL, NT - 1, :], T.x[(NT - 1) * P:N, :]).then_inc(c.x_in[LOADS], 16)
            act.wait_ge(edges_in, 6 * 16)
            for k in range(LOADS):
                act.dma_start(X[:, k * PER:(k + 1) * PER, :],
                              T.x[k * PER * P:(k + 1) * PER * P, :].rearrange("(t p) f -> p t f", p=P)).then_inc(c.x_in[k], 16)

        @block.gpsimd
        def _(pool):
            nc.gpsimd.iota(c.iota[:, :], pattern=[[1, EG]], base=0, channel_multiplier=0,
                           allow_small_or_imprecise_dtypes=True).then_inc(iotas, 1)
            nc.gpsimd.iota(part[:, :], pattern=[[0, 1]], base=0, channel_multiplier=1,
                           allow_small_or_imprecise_dtypes=True).then_inc(iotas, 1)

        @block.vector
        def _(v):
            done = [0]

            def link(ins):
                done[0] += 1
                ins.then_inc(dve, 1)
                v.wait_ge(dve, done[0])
            nc.vector.memset(X[:, NT - 1, :], 0.0).then_inc(tail_set, 1)
            nc.vector.memset(dst_i[:, NCH - 1, :], PAD_DST).then_inc(pads_set, 1)
            nc.vector.memset(src_i[:, NCH - 1, :], 0).then_inc(pads_set, 1)
            nc.vector.memset(start[:, :, 0:1], 0.0)
            nc.vector.memset(end[:, :, P - 1:P], 1.0)
            nc.vector.memset(ones[:, :], 1.0)
            v.wait_ge(iotas, 2)
            nc.vector.tensor_scalar(c.ident[:, :], iota_row, part[:, 0:1], None, ALU.is_equal).then_inc(consts, 1)
            link(nc.vector.tensor_scalar(limit[:, :], part[:, :], 1.0, float(P), ALU.add, ALU.mult))
            v.wait_ge(edges_in, 6 * 16)
            nc.vector.tensor_copy(dst_s[:, :, :], dst_i[:, :, :]).then_inc(shorts_set, 1)
            link(nc.vector.tensor_copy(dst_f[:, :, :], dst_i[:, :, :]))
            link(nc.vector.tensor_copy(src_f[:, :, :], src_i[:, :, :]))
            link(nc.vector.tensor_tensor(end[:, :, 0:P - 1], dst_f[:, :, 1:P], dst_f[:, :, 0:P - 1], ALU.not_equal))
            nc.vector.tensor_scalar(start[:, :, 1:P], end[:, :, 0:P - 1], -BIG, None, ALU.mult).then_inc(flags_set, 1)
            for k in range(NCH):
                v.wait_ge(transposed, k + 1)
                rows = slice(k * P // G, (k + 1) * P // G)
                bank = ps[:, k % 2, 0:3 * P].rearrange("p (w a t) -> p w a t", w=3, t=G)
                nc.vector.tensor_copy(meta_i[:, rows, 0:G], bank[:, 0]).then_inc(meta_built, 1)
                nc.vector.tensor_copy(meta[:, rows, G:2 * G], bank[:, 1]).then_inc(meta_built, 1)
                nc.vector.tensor_copy(meta[:, rows, 2 * G:3 * G], bank[:, 2]).then_inc(meta_built, 1)
            for k in range(LOADS):
                v.wait_ge(c.x_in[k], 16)
                with v.Fori(k * PER // 4, (k + 1) * PER // 4) as q:
                    for j in range(4):
                        nc.vector.bn_stats(c.stats[:, bass.ds(4 * q + j, 1), :].rearrange("p a b -> p (a b)"),
                                           X[:, bass.ds(4 * q + j, 1), :].rearrange("p a b -> p (a b)")).then_inc(normed, 1)
            v.wait_ge(c.x_in[LOADS], 16)
            nc.vector.bn_stats(c.stats[:, NT - 1, :], X[:, NT - 1, :]).then_inc(normed, 1)
            v.wait_ge(last_in, 16)
            link(nc.vector.tensor_scalar(less[:, :], last[:, :, 2 * G - 1], limit[0:NT - 1, 0:1], None, ALU.is_lt))
            link(nc.vector.tensor_reduce(turn[0:NT - 1, :], less[:, :], AX, ALU.add))
            link(nc.vector.tensor_scalar(turn[0:NT - 1, :], turn[0:NT - 1, :], part[0:NT - 1, 0:1], 1.0, ALU.add, ALU.add))
            nc.vector.tensor_scalar(reach[:, :], c.iota[0:NT - 1, 0:NS], turn[0:NT - 1, 0:1], None, ALU.is_ge).then_inc(reached, 1)
            v.wait_ge(nt_counted, 1)
            link(nc.vector.tensor_copy(nt_f[:, :], ps[:, 2, 0:NS]))
            link(nc.vector.tensor_scalar(c.win_base[:, :], nt_f[:, :], float(P), None, ALU.mult))
            link(nc.vector.memset(c.win_new[:, 0:1], 0.0))
            link(nc.vector.tensor_tensor(c.win_new[:, 1:NS], nt_f[:, 1:NS], nt_f[:, 0:NS - 1], ALU.not_equal))
            link(nc.vector.tensor_scalar(c.win_new[:, 1:NS], c.win_new[:, 1:NS], -2.0 * BIG, None, ALU.mult))
            link(nc.vector.tensor_scalar(part[:, :], part[:, :], -1.0, None, ALU.mult))
            link(nc.vector.tensor_scalar(c.win_nodes[:, :], nt_f[:, :], -float(P), part[:, 0:1], ALU.mult, ALU.add))
            link(nc.vector.tensor_copy(c.nt_row[0:1, 0:NS], nt_f[0:1, :]))
            link(nc.vector.tensor_tensor(ea_f[:, :], c.iota[0:1, 0:NS], nt_f[0:1, :], ALU.subtract))
            link(nc.vector.tensor_copy(c.ea_row[0:1, 0:NS], ea_f[:, :]))
            v.wait_ge(normed, NT)

        @block.tensor
        def _(pe):
            pe.wait_ge(consts, 1)
            pe.wait_ge(flags_set, 1)
            for k in range(NCH):
                if k >= 2:
                    pe.wait_ge(meta_built, 3 * (k - 1))
                for w, tile in enumerate((src_f, dst_f, end)):
                    t = nc.tensor.transpose(ps[:, k % 2, w * P:(w + 1) * P], tile[:, k, :], c.ident[:, :])
                t.then_inc(transposed, 1)
            pe.wait_ge(reached, 1)
            nc.tensor.matmul(ps[:, 2, 0:NS], ones[:, :], reach[:, :], start=True, stop=True).then_inc(nt_counted, 1)


def feature_phase(nc, T):
    c = T.c
    at = c.base
    c.q = carve(T.arena, at, [P, NTE, F]); at += NTE * F
    wall = carve(T.arena, at, [P, 2, 3 * F]); at += 6 * F
    hT = carve(T.arena, at, [P, 2, F]); at += 2 * F
    kv = carve(T.arena, at, [P, 2, 2 * F]); at += 4 * F
    hs = carve(T.arena, at, [P, 2, F]); at += 2 * F
    stats = c.stats
    half = carve(T.arena, at, [P, NT]); at += NT
    mean = carve(T.arena, at, [P, NT]); at += NT
    var = carve(T.arena, at, [P, NT]); at += NT
    rstd = carve(T.arena, at, [P, NT]); at += NT
    std = carve(T.arena, at, [P, NT]); at += NT
    nmr = carve(T.arena, at, [P, NT]); at += NT
    X = c.acc[:, 0:NT * F].rearrange("p (t f) -> p t f", f=F)
    ps = T.psum
    with ExitStack() as ctx:
        def sem(name):
            return ctx.enter_context(nc.semaphore(name))
        w_in = sem("w_in")
        sdve, h_ready, hT_ps, hT_ready, q_ps, kv_ps = sem("fdve"), sem("h_ready"), sem("hT_ps"), sem("hT_ready"), sem("q_ps"), sem("kv_ps")
        q_ready, kv_ready, h_out, acc_clear = sem("q_ready"), sem("kv_ready"), [sem("h_out0"), sem("h_out1")], sem("acc_clear")
        kv_out = [sem("kv_out0"), sem("kv_out1")]
        var_ready, std_ready, norm_ready = sem("var_ready"), sem("std_ready"), sem("norm_ready")
        block = ctx.enter_context(nc.Block())

        def tiles(eng, body):
            body(0, 0, 0)
            body(1, 1, 0)
            with eng.Fori(1, (NT - 3) // 2) as i:
                body(2 * i, 0, i)
                body(2 * i + 1, 1, i)
            for t in range(NT - 3, NT):
                body(t, t % 2, t // 2)

        def has(t):
            return not isinstance(t, int) or t < NT

        @block.sync
        def _(sp):
            for j, w in enumerate((T.Wq, T.Wk, T.Wv)):
                sp.dma_start(wall[:, :, j * F:(j + 1) * F], w.rearrange("(k p) n -> p k n", p=P)).then_inc(w_in, 16)

            def store_h(t, b):
                sp.wait_ge(h_ready, t + 1)
                sp.dma_start(T.h_tab[bass.ds(t * P, P), :], hs[:, b, :]).then_inc(h_out[b], 16)
            store_h(0, 0)
            store_h(1, 1)

            def body(t, b, turn):
                if has(t + 2):
                    store_h(t + 2, b)
                sp.wait_ge(kv_ready, t + 1)
                rows = T.kv_tab[bass.ds(t * P, P), :]
                sp.dma_start(rows, kv[:, b, :]).then_inc(kv_out[b], 16)
            tiles(sp, body)
            for stored in (h_out, kv_out):
                sp.wait_ge(stored[0], 16 * (NT // 2 + 1))
                sp.wait_ge(stored[1], 16 * (NT // 2))

        @block.vector
        def _(v):
            done = [0]

            def link(ins):
                done[0] += 1
                ins.then_inc(sdve, 1)
                v.wait_ge(sdve, done[0])
            me, mo, se, so = (stats[:, :, j] for j in (1, 4, 2, 5))
            link(nc.vector.tensor_tensor(mean[:, :], me, mo, ALU.add))
            link(nc.vector.tensor_scalar(mean[:, :], mean[:, :], 0.5, None, ALU.mult))
            link(nc.vector.tensor_tensor(half[:, :], me, mean[:, :], ALU.subtract))
            link(nc.vector.tensor_tensor(half[:, :], half[:, :], half[:, :], ALU.mult))
            link(nc.vector.tensor_tensor(var[:, :], se, so, ALU.add))
            link(nc.vector.scalar_tensor_tensor(var[:, :], var[:, :], 1.0 / F, half[:, :], ALU.mult, ALU.add))
            nc.vector.tensor_scalar(var[:, :], var[:, :], EPS, None, ALU.add).then_inc(var_ready, 1)
            v.wait_ge(std_ready, 1)
            link(nc.vector.reciprocal(rstd[:, :], std[:, :]))
            nc.vector.scalar_tensor_tensor(nmr[:, :], mean[:, :], -1.0, rstd[:, :], ALU.mult, ALU.mult).then_inc(norm_ready, 1)

            def copy_hT(t, b):
                v.wait_ge(hT_ps, t + 1)
                wait(v, q_ps, t - 1)
                wait(v, kv_ps, t - 1)
                nc.vector.tensor_copy(hT[:, b, :], ps[:, b, 0:F]).then_inc(hT_ready, 1)
            copy_hT(0, 0)

            def body(t, b, turn):
                if has(t + 1):
                    copy_hT(t + 1, 1 - b)
                v.wait_ge(kv_ps, t + 1)
                wait(v, kv_out[b], 16 * turn)
                nc.vector.tensor_copy(kv[:, b, :], ps[:, 4 + b, :]).then_inc(kv_ready, 1)
            tiles(v, body)

        @block.gpsimd
        def _(pool):
            for k in range(LOADS):
                pool.wait_ge(h_ready, (k + 1) * PER)
                nc.gpsimd.memset(c.acc[:, k * PER * F:(k + 1) * PER * F], 0.0).then_inc(acc_clear, 1)
            pool.wait_ge(h_ready, NT)
            nc.gpsimd.memset(c.acc[:, LOADS * PER * F:NTE * H * W], 0.0).then_inc(acc_clear, 1)
            pool.wait_ge(acc_clear, LOADS + 1)

        @block.scalar
        def _(act):
            act.wait_ge(var_ready, 1)
            nc.scalar.activation(std[:, :], var[:, :], ACT.Sqrt).then_inc(std_ready, 1)
            act.wait_ge(norm_ready, 1)

            def make_h(t, b, turn):
                wait(act, hT_ps, t - 1)
                wait(act, h_out[b], 16 * turn)
                nc.scalar.activation(hs[:, b, :], X[:, bass.ds(t, 1), :].rearrange("p a b -> p (a b)"), ACT.Relu,
                                     bias=nmr[:, bass.ds(t, 1)], scale=rstd[:, bass.ds(t, 1)]).then_inc(h_ready, 1)
            make_h(0, 0, 0)
            make_h(1, 1, 0)

            def body(t, b, turn):
                if has(t + 2):
                    make_h(t + 2, b, turn + 1)
                act.wait_ge(q_ps, t + 1)
                nc.scalar.activation(c.q[:, bass.ds(t, 1), :].rearrange("p a b -> p (a b)"), ps[:, 2 + b, 0:F],
                                     ACT.Copy, scale=SCALE).then_inc(q_ready, 1)
            tiles(act, body)

        @block.tensor
        def _(pe):
            pe.wait_ge(w_in, 48)

            def transpose_h(t, b):
                pe.wait_ge(h_ready, t + 1)
                wait(pe, hT_ready, t - 1)
                for k in range(2):
                    m = nc.tensor.transpose(ps[:, b, k * P:(k + 1) * P],
                                            hs[:, b, k * P:(k + 1) * P], c.ident[:, :])
                m.then_inc(hT_ps, 1)
            transpose_h(0, 0)

            def body(t, b, turn):
                if has(t + 1):
                    transpose_h(t + 1, 1 - b)
                pe.wait_ge(hT_ready, t + 1)
                wait(pe, q_ready, t - 1)
                for k in range(2):
                    m = nc.tensor.matmul(ps[:, 2 + b, 0:F], hT[:, b, k * P:(k + 1) * P], wall[:, k, 0:F], start=(k == 0), stop=(k == 1))
                m.then_inc(q_ps, 1)
                wait(pe, kv_ready, t - 1)
                for k in range(2):
                    m = nc.tensor.matmul(ps[:, 4 + b, :], hT[:, b, k * P:(k + 1) * P], wall[:, k, F:3 * F], start=(k == 0), stop=(k == 1))
                m.then_inc(kv_ps, 1)
            tiles(pe, body)


def edge_phase(nc, T):
    c = T.c
    at = c.base + NTE * F

    def take(shape, dt=fp32):
        nonlocal at
        size = 1
        for n in shape[1:]:
            size *= n
        at += size
        return carve(T.arena, at - size, shape, dt)
    kv = take([P, U, G * 2 * F]).rearrange("p u (g f) -> p u g f", g=G)
    nodes = carve(T.arena, at, [P, U, EG // 2]).rearrange("p u f -> p (u f)").bitcast(i16).rearrange("p (u f) -> p u f", u=U)
    at += U * EG // 2
    hot_w = take([P, U, EG])
    hot_e = take([P, U, EG]).rearrange("p u (g w) -> p u g w", g=G)
    meta = take([P, U, 3 * G])
    flags = take([16, U, P])
    prod = take([P, G, F])
    pv = take([P, U, G * H * W]).rearrange("p u (g h w) -> p u g h w", g=G, h=H)
    score = take([P, 2, G * H])
    runmax = take([16, P])
    ends = take([P, G, H + 1])
    absent = take([P, G])
    local = take([P, G])
    grpmax = take([P, G, H])
    topmax = take([P, H])
    newmax = take([P, 2, H])
    fall = take([P, U, H])
    shift = take([P, U, G * H])
    decay = take([P, U, H])
    assert at <= 52600, at
    ps = T.psum
    qe = [ps[:, 2 * b:2 * b + 2, :].rearrange("p b (g f) -> p (b g) f", f=F) for b in range(2)]
    sums = [ps[:, 4 + b, 0:H * W] for b in range(2)]
    scoreT = ps[0:16, 6, 0:P]
    endsT = ps[:, 6, P:P + 16]
    grp = ps[:, 7, 0:G * (H + 1)].rearrange("p (g k) -> p g k", g=G)
    ref = ps[:, 7, 64:64 + G * H]
    acc = c.acc.rearrange("p (t h w) -> p t h w", h=H, w=W)
    LAST = NS + 5

    with ExitStack() as ctx:
        def sem(name):
            return ctx.enter_context(nc.semaphore(name))
        meta_in = [sem(f"meta_in{u}") for u in range(U)]
        rows_in = [sem(f"rows_in{u}") for u in range(U)]
        kv_in = [sem(f"kv_in{u}") for u in range(U)]
        hot_w_ready, hot_e_ready, ends_ready, prod_ready = sem("hot_w_ready"), sem("hot_e_ready"), sem("ends_ready"), sem("prod_ready")
        max_link, max_ready, score_ready, shift_ready = sem("max_link"), sem("max_ready"), sem("score_ready"), sem("shift_ready")
        distance_ready = sem("distance_ready")
        local_ready = sem("local_ready")
        gather_begins, turn_begins = sem("gather_begins"), sem("turn_begins")
        scan_ready, added = sem("scan_ready"), sem("added")
        qe_ready, grp_ready, ref_ready, scoreT_ready, endsT_ready, sums_ready = (
            sem(n) for n in ("qe_ready", "grp_ready", "ref_ready", "scoreT_ready", "endsT_ready", "sums_ready"))
        p_ready, pv_ready, top_set = sem("p_ready"), sem("pv_ready"), sem("top_set")
        block = ctx.enter_context(nc.Block())

        def loop(eng, total, body):
            whole = total // U
            for i in range(2 * U):
                body(i, i % U, i // U)
            with eng.Fori(2, whole - 2) as k:
                for u in range(U):
                    body(U * k + u, u, k)
            for i in range((whole - 2) * U, total):
                body(i, i % U, i // U)

        def load(eng, row, s):
            return eng.value_load(row[0:1, bass.ds(s, 1)] if not isinstance(s, int) else row[0:1, s:s + 1],
                                  min_val=0, max_val=NG - 1 if row is c.ea_row else NT - 1)

        @block.sync
        def _(sp):
            def body(s, u, turn):
                ea = load(sp, c.ea_row, s)
                wait(sp, ends_ready, s - U + 1)
                sp.dma_start(meta[:, u, :], T.meta_tab[:, bass.ds(ea * (3 * G), 3 * G)]).then_inc(meta_in[u], 16)
                wait(sp, hot_w_ready, s - U + 1)
                sp.dma_start(nodes[:, u, :], T.dst_pad[bass.ds(ea * EG, EG)].partition_broadcast(P)).then_inc(rows_in[u], 16)
                sp.dma_start(flags[:, u, :], T.flag_tab[bass.ds(ea * G, G), :].unsqueeze(1).broadcast_to([G, H, P])).then_inc(rows_in[u], 16)
            loop(sp, NS, body)

        @block.gpsimd
        def _(pool):
            def body(s, u, turn):
                pool.wait_ge(meta_in[u], 16 * (turn + 1))
                wait(pool, pv_ready, s - U + 1)
                pool.sem_inc(gather_begins, 1)
                for g in range(G):
                    pool.indirect_dma_start(out=kv[:, u, g, :], out_offset=None, in_=T.kv_tab[:, :],
                                            in_offset=bass.IndirectOffsetOnAxis(ap=meta[:, u, g:g + 1].bitcast(i32), axis=0),
                                            ).then_inc(kv_in[u], 16)
            loop(pool, NS, body)

        @block.vector
        def _(v):
            links = 4

            nc.vector.memset(newmax[:, :, :], -BIG).then_inc(top_set, 1)
            def body(i, u, turn):
                one = isinstance(i, int)
                u1 = (u - 1) % U
                if not one or 1 <= i <= NS:
                    v.wait_ge(endsT_ready, i)
                    nc.vector.tensor_tensor(ends[:, :, 0:H], endsT.rearrange("p (g h) -> p g h", g=G),
                                            bcast(meta[:, u1, 2 * G:3 * G].unsqueeze(2), 2, H), ALU.mult).then_inc(ends_ready, 1)
                if not one or i < NS:
                    v.wait_ge(qe_ready, i + 1)
                    v.wait_ge(kv_in[u], 64 * (turn + 1))
                    nc.vector.tensor_tensor(prod[:, :, :], kv[:, u, :, 0:F], qe[u % 2], ALU.mult).then_inc(prod_ready, 1)
                window = load(v, c.nt_row, i - 5) if not one or i >= 5 else None
                fresh, flush = not one or 1 <= i <= NS, not one or i >= 5
                def add_head(h):
                    if flush:
                        a = acc[:, bass.ds(window, 1), h, :].rearrange("p a w -> p (a w)")
                        m = nc.vector.scalar_tensor_tensor(a, a, decay[:, u1, h:h + 1], sums[(u + 1) % 2][:, h * W:(h + 1) * W], ALU.mult, ALU.add)
                        if h == H - 1:
                            m.then_inc(added, 1)
                if fresh:
                    v.wait_ge(grp_ready, i)
                    n0 = links * (i - 1)
                    nc.vector.tensor_scalar(absent[:, :], grp[:, :, H], BIG, None, ALU.subtract).then_inc(max_link, 1)
                if fresh:
                    v.wait_ge(max_link, n0 + 1)
                    nc.vector.tensor_tensor(grpmax[:, :, :], grp[:, :, 0:H], bcast(absent[:, :].unsqueeze(2), 2, H), ALU.add).then_inc(max_link, 1)
                if flush and one and i > NS:
                    v.wait_ge(sums_ready, i - 4)
                    v.wait_ge(added, i - 5)
                add_head(0)
                if fresh:
                    v.wait_ge(max_link, n0 + 2)
                    nc.vector.tensor_reduce(topmax[:, :], grpmax[:, :, :].rearrange("p g h -> p h g"), AX, ALU.max).then_inc(max_link, 1)
                add_head(1)
                if fresh:
                    v.wait_ge(max_link, n0 + 3)
                    now, before = newmax[:, (u + 1) % 2, :], newmax[:, u % 2, :]
                    new = c.win_new[:, bass.ds(i - 1, 1)]
                    nc.vector.scalar_tensor_tensor(now, before, new, topmax[:, :], ALU.add, ALU.max).then_inc(max_link, 1)
                add_head(2)
                if fresh:
                    v.wait_ge(max_link, n0 + 4)
                    nc.vector.scalar_tensor_tensor(fall[:, u1, :], before, new, now, ALU.add, ALU.subtract).then_inc(max_ready, 1)
                add_head(3)
                if not one or i < NS:
                    v.wait_ge(prod_ready, i + 1)
                    nc.vector.tensor_reduce(score[:, u % 2, :], prod[:, :, :].rearrange("p g (h d) -> p (g h) d", h=H), AX, ALU.add).then_inc(score_ready, 1)
                if not one or 1 <= i <= NS:
                    v.wait_ge(ref_ready, i)
                    nc.vector.tensor_tensor(shift[:, u1, :], score[:, (u + 1) % 2, :], ref, ALU.subtract).then_inc(shift_ready, 1)
                if not one or i < NS:
                    nc.vector.tensor_scalar(local[:, :], meta[:, u, G:2 * G], c.win_base[:, bass.ds(i, 1)], None, ALU.subtract).then_inc(local_ready, 1)
                    nc.vector.tensor_scalar(ends[:, :, H:H + 1], meta[:, u, 2 * G:3 * G].unsqueeze(2), BIG, None, ALU.mult)
                    v.wait_ge(scoreT_ready, i + 1)
                    nc.vector.tensor_tensor_scan(runmax[:, :], flags[:, u, :], scoreT, -BIG, ALU.add, ALU.max).then_inc(scan_ready, 1)
                    wait(v, sums_ready, i - U + 1)
                    v.wait_ge(local_ready, i + 1)
                    nc.vector.tensor_tensor(hot_e[:, u, :, :], bcast(c.iota[:, 0:P].unsqueeze(1), 1, G),
                                            bcast(local[:, :].unsqueeze(2), 2, P), ALU.is_equal).then_inc(hot_e_ready, 1)
            v.wait_ge(top_set, 1)
            loop(v, LAST, body)

        @block.scalar
        def _(act):
            def distance(s, u, turn):
                act.wait_ge(rows_in[u], 32 * (turn + 1))
                nc.scalar.activation(hot_w[:, u, :], nodes[:, u, :], ACT.Square, bias=c.win_nodes[:, bass.ds(s, 1)]).then_inc(distance_ready, 1)

            def build_hot_w(s, u):
                act.wait_ge(distance_ready, s + 1)
                nc.scalar.activation(hot_w[:, u, :], hot_w[:, u, :], ACT.Relu, bias=1.0, scale=-1.0).then_inc(hot_w_ready, 1)
            for s in range(U):
                distance(s, s, 0)
                build_hot_w(s, s)

            def body(s, u, turn):
                act.wait_ge(shift_ready, s + 1)
                nc.scalar.activation(pv[:, u, :, :, D:W].rearrange("p g h w -> p (g h w)"), shift[:, u, :], ACT.Exp).then_inc(p_ready, 1)
                nc.scalar.activation(decay[:, u, :], fall[:, u, :], ACT.Exp)
                more = not isinstance(s, int) or s + U < NS
                act.wait_ge(p_ready, s + 1)
                for g in range(G):
                    if more and g == G // 2:
                        distance(s + U, u, turn + 1)
                    for h in range(H):
                        m = nc.scalar.activation(pv[:, u, g, h, 0:D], kv[:, u, g, F + h * D:F + (h + 1) * D], ACT.Copy,
                                                 scale=pv[:, u, g, h, D:W])
                m.then_inc(pv_ready, 1)
                if more:
                    build_hot_w(s + U, u)
            loop(act, NS, body)

        @block.tensor
        def _(pe):
            def queries(s, u, window):
                pe.wait_ge(hot_w_ready, s + 1)
                qw = c.q[:, bass.ds(window, 1), :].rearrange("p a f -> p (a f)")
                for g in range(G):
                    m = nc.tensor.matmul(qe[u % 2][:, g, :], hot_w[:, u, g * P:(g + 1) * P], qw, start=True, stop=True)
                m.then_inc(qe_ready, 1)

            def body(i, u, turn):
                one = isinstance(i, int)
                u1, u3 = (u - 1) % U, (u - 3) % U

                def sum_tiles(su, tiles):
                    for g in tiles:
                        m = nc.tensor.matmul(sums[su % 2], hot_e[:, su, g, :], pv[:, su, g, :, :].rearrange("p h w -> p (h w)"),
                                             start=(g == 0), stop=(g == G - 1))
                        if g == G - 1:
                            m.then_inc(sums_ready, 1)
                if one and i == 0:
                    queries(0, 0, load(pe, c.nt_row, 0))
                if not one or 1 <= i <= NS:
                    pe.wait_ge(ends_ready, i)
                    for g in range(G):
                        m = nc.tensor.matmul(grp[:, g, :], hot_e[:, u1, g, :], ends[:, g, :], start=True, stop=True)
                    m.then_inc(grp_ready, 1)
                if not one or i + 1 < NS:
                    queries(i + 1, (u + 1) % U, load(pe, c.nt_row, i + 1))
                if not one or 1 <= i <= NS:
                    pe.wait_ge(max_ready, i)
                    for g in range(G):
                        m = nc.tensor.matmul(ref[:, g * H:(g + 1) * H], hot_w[:, u1, g * P:(g + 1) * P], newmax[:, (u + 1) % 2, :], start=True, stop=True)
                    m.then_inc(ref_ready, 1)
                if not one or 4 <= i < NS + 4:
                    sum_tiles(u, range(G - 1, G))
                if not one or i < NS:
                    pe.wait_ge(score_ready, i + 1)
                    nc.tensor.transpose(scoreT, score[:, u % 2, :], c.ident[:, :]).then_inc(scoreT_ready, 1)
                due = not one or 3 <= i < NS + 3
                if due:
                    pe.wait_ge(pv_ready, i - 2)
                    if one and i >= NS:
                        pe.wait_ge(added, i - 4)
                    sum_tiles(u3, range(0, G // 2))
                if not one or i < NS:
                    pe.wait_ge(scan_ready, i + 1)
                    pe.sem_inc(turn_begins, 1)
                    nc.tensor.transpose(endsT, runmax[:, :], c.ident[0:16, 0:16]).then_inc(endsT_ready, 1)
                if due:
                    sum_tiles(u3, range(G // 2, G - 1))
            loop(pe, LAST, body)


def node_phase(nc, T):
    c = T.c
    at = c.base

    def take(shape, dt=fp32):
        nonlocal at
        size = 1
        for n in shape[1:]:
            size *= n
        at += size
        return carve(T.arena, at - size, shape, dt)
    KF, KH = F // P, HID // P
    w1 = take([P, KF, HID])
    w2 = take([P, KH, F])
    wx = take([P, KF, F + 2 * H])
    att = take([P, 2, F])
    attw = take([P, F])
    gain, shift, b2 = take([P, F]), take([P, F]), take([P, F])
    b1, slope = take([P, KH]), take([P, KH])
    c.edge_src = take([P, NT], i32)
    c.edge_dst = take([P, NT], i32)
    rden = take([P, NT, H])
    hin, xin = take([P, 2, F]), take([P, 2, F])
    r = take([P, 2, F])
    rst = take([P, 2, F])
    rstT = take([P, KF, P])
    hid = take([P, 2, KH, P])
    above, below = take([P, KH, P]), take([P, KH, P])
    b1n = take([P, KH])
    y = take([P, 2, F])
    z = take([P, F])
    h2T = take([P, KF, P])
    xt = take([P, 2, F + 2 * H])
    stA, stC, stD = take([P, 6]), take([P, 6]), take([P, 6])
    mvA, mvC, mvD = take([P, 2]), take([P, 2]), take([P, 2])
    sdA, sdC, sdD, eps = take([P, 1]), take([P, 1]), take([P, 1]), take([P, 1])
    assert at <= 52600, at
    ps = T.psum
    rstT_ps, h2T_ps = ps[:, 0, 0:F], ps[:, 4, 0:F]
    hid_ps = ps[:, 1:3, :].rearrange("p b (k n) -> p (b k) n", n=P)
    ffn_ps, xt_ps = ps[:, 3, 0:F], ps[:, 5, 0:F + 2 * H]
    acc4 = c.acc.rearrange("p (t h w) -> p t h w", h=H, w=W)
    accF = c.acc.rearrange("p (t f) -> p t f", f=H * W)

    def tile_of(view, t):
        return view[:, bass.ds(t, 1), :].rearrange("p a f -> p (a f)")

    with ExitStack() as ctx:
        def sem(name):
            return ctx.enter_context(nc.semaphore(name))
        w_in, idx_in, x_clear, setup = sem("w_in"), sem("idx_in"), sem("x_clear"), sem("setup")
        h_in, x_in = [sem("h_in0"), sem("h_in1")], [sem("x_in0"), sem("x_in1")]
        xt_out = [sem("xt_out0"), sem("xt_out1")]
        scaled, summed, r_normed, rst_gain, rst_ready, rb_ready = (
            sem(n) for n in ("scaled", "summed", "r_normed", "rst_gain", "rst_ready", "rb_ready"))
        y_ready, y_normed, y_gain, y_shift, x2_ready, z_ready = (
            sem(n) for n in ("y_ready", "y_normed", "y_gain", "y_shift", "x2_ready", "z_ready"))
        st_A, st_C, st_D, var_A, var_C, var_D = (sem(n) for n in ("stats_a", "stats_c", "stats_d", "var_a", "var_c", "var_d"))
        std_A, std_C, std_D, inv_A, inv_C, inv_D = (sem(n) for n in ("std_a", "std_c", "std_d", "inv_a", "inv_c", "inv_d"))
        rstT_ready, h2T_ready, hid_ready, xt_ready, halves = (sem(n) for n in ("rstT_ready", "h2T_ready", "hid_ready", "xt_ready", "halves"))
        rstT_mm, hid_mm, ffn_mm, h2T_mm, xt_mm = (sem(n) for n in ("rstT_mm", "hid_mm", "ffn_mm", "h2T_mm", "xt_mm"))
        stats_begun = sem("stats_begun")
        block = ctx.enter_context(nc.Block())

        def loop(eng, body):
            for j in range(6):
                body(j, j % 2, j // 2)
            with eng.Fori(3, (NT - 3) // 2) as k:
                body(2 * k, 0, k)
                body(2 * k + 1, 1, k)
            for j in range(NT - 3, NT + 4):
                body(j, j % 2, j // 2)

        def window(j, back):
            return not isinstance(j, int) or back <= j < NT + back

        @block.sync
        def _(sp):
            for tile, src in ((w1, T.W1.rearrange("(k p) n -> p k n", p=P)), (w2, T.W2.rearrange("(k p) n -> p k n", p=P)),
                              (wx[:, :, 0:F], T.weight.rearrange("(k p) n -> p k n", p=P)),
                              (att[:, 0, :], T.attn_r.rearrange("h d -> (h d)").partition_broadcast(P)),
                              (att[:, 1, :], T.attn_l.rearrange("h d -> (h d)").partition_broadcast(P)),
                              (gain, T.ln_g.partition_broadcast(P)), (shift, T.ln_b.partition_broadcast(P)), (b2, T.b2.partition_broadcast(P)),
                              (b1, T.b1.rearrange("(k p) -> p k", p=P)), (slope, T.alpha.rearrange("(k p) -> p k", p=P))):
                sp.dma_start(tile, src, allow_slow_non_contiguous=True).then_inc(w_in, 16)

            def load_h(t, b):
                sp.dma_start(hin[:, b, :], T.h_tab[bass.ds(t * P, P), :]).then_inc(h_in[b], 16)

            def load_x(t, b):
                if isinstance(t, int) and t == NT - 1:
                    sp.dma_start(xin[0:TAIL, b, :], T.x[t * P:N, :]).then_inc(x_in[b], 16)
                else:
                    sp.dma_start(xin[:, b, :], T.x[bass.ds(t * P, P), :]).then_inc(x_in[b], 16)
            load_h(0, 0)
            load_h(1, 1)
            sp.dma_start(c.edge_src, T.src[0:NT * P].rearrange("(t p) -> p t", p=P), allow_slow_non_contiguous=True).then_inc(idx_in, 16)
            sp.dma_start(c.edge_dst, T.dst[0:NT * P].rearrange("(t p) -> p t", p=P), allow_slow_non_contiguous=True).then_inc(idx_in, 16)

            def body(j, b, turn):
                if window(j, -2):
                    sp.wait_ge(summed, j + 1)
                    load_h(j + 2, b)
                if window(j, 2):
                    sp.wait_ge(x_clear, 1)
                    wait(sp, x2_ready, j - 3)
                    load_x(j - 2, b)
                if window(j, 4):
                    sp.wait_ge(xt_ready, j - 3)
                    store(j - 4, b)

            def store(t, b):
                sp.dma_start(T.xt_tab[bass.ds(t * P, P), :], xt[:, b, 0:F + H]).then_inc(xt_out[b], 16)
                sp.dma_start(T.al_tab[bass.ds(t * P, P), :], xt[:, b, F + H:F + 2 * H]).then_inc(xt_out[b], 16)
            loop(sp, body)
            sp.wait_ge(idx_in, 32)
            sp.wait_ge(xt_out[0], 32 * (NT // 2 + 1))
            sp.wait_ge(xt_out[1], 32 * (NT // 2))

        @block.vector
        def _(v):
            done = [0]

            def link(ins):
                done[0] += 1
                ins.then_inc(setup, 1)
                v.wait_ge(setup, done[0])
            nc.vector.memset(xin[:, :, :], 0.0).then_inc(x_clear, 1)
            link(nc.vector.tensor_scalar(rden, acc4[:, 0:NT, :, D], 1.0e-30, None, ALU.max))
            link(nc.vector.reciprocal(rden, rden))
            v.wait_ge(w_in, 16 * 10)
            link(nc.vector.memset(eps, EPS))
            link(nc.vector.tensor_scalar(b1n, b1, -1.0, None, ALU.mult))
            link(nc.vector.tensor_scalar(slope, slope, -1.0, None, ALU.mult))
            for k in range(KF):
                for d in range(2):
                    link(nc.vector.tensor_tensor(attw, wx[:, k, 0:F], att[:, d, :], ALU.mult))
                    link(nc.vector.tensor_reduce(wx[:, k, F + d * H:F + (d + 1) * H], attw.rearrange("p (h d) -> p h d", h=H), AX, ALU.add))

            def average(st, mv, st_sem, var_sem, t):
                v.wait_ge(st_sem, t + 1)
                v.sem_inc(stats_begun, 1)
                nc.vector.bn_aggr(mv, st).then_inc(var_sem, 1)

            def invert(sd, std_sem, inv_sem, t):
                v.wait_ge(std_sem, t + 1)
                nc.vector.reciprocal(sd, sd).then_inc(inv_sem, 1)

            def body(j, b, turn):
                a, hidden, c2, d1 = window(j, 0), window(j, 1), window(j, 3), window(j, 4)
                ra, yc = r[:, b, :], y[:, 1 - b, :]
                if a:
                    wait(v, rst_ready, j - 1)
                    nc.vector.tensor_tensor(ra.rearrange("p (h d) -> p h d", h=H),
                                            acc4[:, bass.ds(j, 1), :, 0:D].rearrange("p a h d -> p (a h) d"),
                                            bcast(rden[:, bass.ds(j, 1), :].rearrange("p a h -> p (a h)").unsqueeze(2), 2, D),
                                            ALU.mult).then_inc(scaled, 1)
                if c2:
                    v.wait_ge(rb_ready, j - 2)
                    v.wait_ge(ffn_mm, j - 2)
                    wait(v, x2_ready, j - 4)
                    nc.vector.tensor_tensor(yc, ffn_ps, tile_of(accF[:, :, 0:F], j - 3), ALU.add).then_inc(y_ready, 1)
                if a:
                    v.wait_ge(scaled, j + 1)
                    v.wait_ge(h_in[b], 16 * (turn + 1))
                    nc.vector.tensor_tensor(ra, ra, hin[:, b, :], ALU.add).then_inc(summed, 1)
                if c2:
                    v.wait_ge(y_ready, j - 2)
                    nc.vector.bn_stats(stC, yc).then_inc(st_C, 1)
                if a:
                    v.wait_ge(summed, j + 1)
                    nc.vector.bn_stats(stA, ra).then_inc(st_A, 1)
                if c2:
                    average(stC, mvC, st_C, var_C, j - 3)
                if d1:
                    x2 = tile_of(accF[:, :, 0:F], j - 4)
                    v.wait_ge(x2_ready, j - 3)
                    v.sem_inc(stats_begun, 1)
                    nc.vector.bn_stats(stD, x2).then_inc(st_D, 1)
                if a:
                    average(stA, mvA, st_A, var_A, j)
                if d1:
                    average(stD, mvD, st_D, var_D, j - 4)
                if c2:
                    invert(sdC, std_C, inv_C, j - 3)
                if a:
                    invert(sdA, std_A, inv_A, j)
                if c2:
                    v.wait_ge(inv_C, j - 2)
                    nc.vector.tensor_scalar(yc, yc, mvC[:, 0:1], sdC[:, 0:1], ALU.subtract, ALU.mult).then_inc(y_normed, 1)
                if a:
                    v.wait_ge(inv_A, j + 1)
                    nc.vector.tensor_scalar(ra, ra, mvA[:, 0:1], sdA[:, 0:1], ALU.subtract, ALU.mult).then_inc(r_normed, 1)
                if d1:
                    invert(sdD, std_D, inv_D, j - 4)
                    v.wait_ge(inv_D, j - 3)
                    wait(v, h2T_mm, j - 4)
                    nc.vector.tensor_scalar(z, x2, mvD[:, 0:1], sdD[:, 0:1], ALU.subtract, ALU.mult).then_inc(z_ready, 1)
                if hidden:
                    wait(v, ffn_mm, j - 2)
                    for k in range(KH):
                        v.wait_ge(halves, KH * (j - 1) + k + 1)
                        nc.vector.scalar_tensor_tensor(hid[:, 1 - b, k, :], below[:, k, :], slope[:, k:k + 1], above[:, k, :],
                                                       ALU.mult, ALU.add).then_inc(hid_ready, 1)
            loop(v, body)

        @block.gpsimd
        def _(pool):
            pool.wait_ge(w_in, 16 * 10)

            def body(j, b, turn):
                a, c2 = window(j, 0), window(j, 3)
                ra, yc, ro = r[:, b, :], y[:, 1 - b, :], rst[:, b, :]
                if c2:
                    pool.wait_ge(y_normed, j - 2)
                    nc.gpsimd.tensor_tensor(yc, yc, gain, ALU.mult).then_inc(y_gain, 1)
                if a:
                    pool.wait_ge(r_normed, j + 1)
                    nc.gpsimd.tensor_tensor(ra, ra, gain, ALU.mult).then_inc(rst_gain, 1)
                if c2:
                    pool.wait_ge(y_gain, j - 2)
                    nc.gpsimd.tensor_tensor(yc, yc, shift, ALU.add).then_inc(y_shift, 1)
                if a:
                    pool.wait_ge(rst_gain, j + 1)
                    wait(pool, rstT_mm, j - 1)
                    nc.gpsimd.tensor_tensor(ro, ra, shift, ALU.add).then_inc(rst_ready, 1)
                if c2:
                    pool.wait_ge(y_shift, j - 2)
                    pool.wait_ge(x_in[1 - b], 16 * (turn - 1 + b))
                    nc.gpsimd.tensor_tensor(tile_of(accF[:, :, 0:F], j - 3), yc, xin[:, 1 - b, :], ALU.add).then_inc(x2_ready, 1)
                if a:
                    pool.wait_ge(rst_ready, j + 1)
                    nc.gpsimd.tensor_tensor(tile_of(accF[:, :, 0:F], j), ro, b2, ALU.add).then_inc(rb_ready, 1)
            loop(pool, body)

        @block.scalar
        def _(act):
            def root(var_sem, mv, sd, ok, t):
                act.wait_ge(var_sem, t + 1)
                nc.scalar.activation(sd, mv[:, 1:2], ACT.Sqrt, bias=eps).then_inc(ok, 1)
            act.wait_ge(setup, 5)

            def relus(t, k):
                act.wait_ge(hid_mm, 2 * t + 1 + k // (KH // 2))
                if k % (KH // 2) == 0:
                    wait(act, hid_ready, KH * (t - 1) + k + KH // 2)
                nc.scalar.activation(above[:, k, :], hid_ps[:, k, :], ACT.Relu, bias=b1[:, k:k + 1])
                nc.scalar.activation(below[:, k, :], hid_ps[:, k, :], ACT.Relu, bias=b1n[:, k:k + 1], scale=-1.0).then_inc(halves, 1)

            def body(j, b, turn):
                if window(j, 3):
                    root(var_C, mvC, sdC, std_C, j - 3)
                if window(j, 0):
                    root(var_A, mvA, sdA, std_A, j)
                if window(j, 4):
                    root(var_D, mvD, sdD, std_D, j - 4)
                if window(j, 1):
                    for k in range(KH // 2):
                        relus(j - 1, k)
                if window(j, 4):
                    act.wait_ge(h2T_mm, j - 3)
                    wait(act, xt_mm, j - 4)
                    nc.scalar.activation(h2T.rearrange("p k n -> p (k n)"), h2T_ps, ACT.Relu).then_inc(h2T_ready, 1)
                if window(j, 1):
                    for k in range(KH // 2, KH):
                        relus(j - 1, k)
                if window(j, 0):
                    act.wait_ge(rstT_mm, j + 1)
                    wait(act, hid_mm, 2 * j)
                    nc.scalar.copy(rstT.rearrange("p k n -> p (k n)"), rstT_ps).then_inc(rstT_ready, 1)
                if window(j, 4):
                    act.wait_ge(xt_mm, j - 3)
                    if not isinstance(j, int) or j >= 6:
                        wait(act, xt_out[b], 32 * (turn - 2))
                    nc.scalar.copy(xt[:, b, :], xt_ps).then_inc(xt_ready, 1)
            loop(act, body)

        @block.tensor
        def _(pe):
            def body(j, b, turn):
                if window(j, 1):
                    pe.wait_ge(rstT_ready, j)
                    for n in range(KH):
                        if n % (KH // 2) == 0:
                            wait(pe, halves, KH * (j - 2) + n + KH // 2)
                        for k in range(KF):
                            m = nc.tensor.matmul(hid_ps[:, n, :], w1[:, k, n * P:(n + 1) * P], rstT[:, k, :], start=(k == 0), stop=(k == KF - 1))
                        if n % (KH // 2) == KH // 2 - 1:
                            m.then_inc(hid_mm, 1)
                if window(j, 4):
                    pe.wait_ge(z_ready, j - 3)
                    wait(pe, h2T_ready, j - 4)
                    for k in range(KF):
                        m = nc.tensor.transpose(h2T_ps[:, k * P:(k + 1) * P], z[:, k * P:(k + 1) * P], c.ident)
                    m.then_inc(h2T_mm, 1)
                if window(j, 2):
                    wait(pe, y_ready, j - 2)
                    for n in range(KH):
                        pe.wait_ge(hid_ready, KH * (j - 2) + n + 1)
                        m = nc.tensor.matmul(ffn_ps, hid[:, b, n, :], w2[:, n, :], start=(n == 0), stop=(n == KH - 1))
                    m.then_inc(ffn_mm, 1)
                if window(j, 0):
                    pe.wait_ge(rst_ready, j + 1)
                    wait(pe, rstT_ready, j)
                    for k in range(KF):
                        m = nc.tensor.transpose(rstT_ps[:, k * P:(k + 1) * P], rst[:, b, k * P:(k + 1) * P], c.ident)
                    m.then_inc(rstT_mm, 1)
                if window(j, 4):
                    pe.wait_ge(h2T_ready, j - 3)
                    wait(pe, xt_ready, j - 4)
                    for k in range(KF):
                        m = nc.tensor.matmul(xt_ps, h2T[:, k, :], wx[:, k, :], start=(k == 0), stop=(k == KF - 1))
                    m.then_inc(xt_mm, 1)
            pe.wait_ge(setup, 5 + 4 * KF)
            loop(pe, body)


def output_phase(nc, T):
    c = T.c
    at = c.base + 12000
    xg = carve(T.arena, at, [P, NT, F + H]); at += NT * (F + H)
    al = carve(T.arena, at, [P, NT, H]); at += NT * H
    sc = carve(T.arena, at, [P, NT, H]); at += NT * H
    mx = carve(T.arena, at, [P, NT]); at += NT
    mixed = carve(T.arena, at, [P, NT, D]); at += NT * D
    assert at <= 52600, at
    accF = c.acc.rearrange("p (t f) -> p t f", f=H * W)
    PER = 7
    PARTS = NT // PER
    with ExitStack() as ctx:
        def sem(name):
            return ctx.enter_context(nc.semaphore(name))
        rows_in = [sem(f"rows_in{k}") for k in range(PARTS)]
        link_sem, shifted, powered, part_ready, stored = sem("link"), sem("shifted"), sem("powered"), sem("part_ready"), sem("stored")
        block = ctx.enter_context(nc.Block())

        @block.gpsimd
        def _(pool):
            for t in range(NT):
                for tab, tile, ids in ((T.al_tab, al[:, t, :], c.edge_src), (T.xt_tab, xg[:, t, :], c.edge_dst)):
                    pool.indirect_dma_start(out=tile, out_offset=None, in_=tab[:, :],
                                            in_offset=bass.IndirectOffsetOnAxis(ap=ids[:, t:t + 1], axis=0)).then_inc(rows_in[t // PER], 16)

        @block.vector
        def _(v):
            done = [0]

            def link(ins):
                done[0] += 1
                ins.then_inc(link_sem, 1)
                v.wait_ge(link_sem, done[0])
            for k in range(PARTS):
                ts = slice(k * PER, (k + 1) * PER)
                s, m = sc[:, ts, :], mx[:, ts]
                v.wait_ge(rows_in[k], 32 * PER)
                link(nc.vector.tensor_tensor(s, al[:, ts, :], xg[:, ts, F:F + H], ALU.add))
                link(nc.vector.scalar_tensor_tensor(s, s, 0.01, s, ALU.mult, ALU.max))
                link(nc.vector.tensor_reduce(m, s, AX, ALU.max))
                nc.vector.tensor_tensor(s, s, bcast(m.unsqueeze(2), 2, H), ALU.subtract).then_inc(shifted, 1)
                v.wait_ge(powered, k + 1)
                link(nc.vector.tensor_reduce(m, s, AX, ALU.add))
                link(nc.vector.reciprocal(m, m))
                link(nc.vector.tensor_tensor(s, s, bcast(m.unsqueeze(2), 2, H), ALU.mult))
                heads = xg[:, ts, 0:F].rearrange("p t (h d) -> p t h d", h=H)
                link(nc.vector.tensor_tensor(heads, heads, bcast(s.unsqueeze(3), 3, D), ALU.mult))
                link(nc.vector.tensor_tensor(heads[:, :, 0:2, :], heads[:, :, 0:2, :], heads[:, :, 2:4, :], ALU.add))
                link(nc.vector.tensor_tensor(mixed[:, ts, :], heads[:, :, 0, :], heads[:, :, 1, :], ALU.add))
                o = accF[:, ts, 0:F].rearrange("p t (h d) -> p t h d", h=H)
                nc.vector.tensor_tensor(o, o, bcast(mixed[:, ts, :].unsqueeze(2), 2, H), ALU.add).then_inc(part_ready, 1)

        @block.scalar
        def _(act):
            for k in range(PARTS):
                s = sc[:, k * PER:(k + 1) * PER, :]
                act.wait_ge(shifted, k + 1)
                nc.scalar.activation(s, s, ACT.Exp).then_inc(powered, 1)

        @block.sync
        def _(sp):
            for k in range(PARTS):
                sp.wait_ge(part_ready, k + 1)
                whole = min((k + 1) * PER, NT - 1)
                sp.dma_start(T.out[k * PER * P:whole * P, :].rearrange("(t p) f -> p t f", p=P), accF[:, k * PER:whole, 0:F]).then_inc(stored, 16)
            sp.dma_start(T.out[(NT - 1) * P:N, :], accF[0:TAIL, NT - 1, 0:F]).then_inc(stored, 16)
            sp.wait_ge(stored, 16 * (PARTS + 1))


_INS = ['x', 'src', 'dst', 'L0_gnn_Wq', 'L0_gnn_Wk', 'L0_gnn_Wv', 'L0_gnn_ln_g', 'L0_gnn_ln_b', 'L0_gnn_W1', 'L0_gnn_b1',
        'L0_gnn_alpha', 'L0_gnn_W2', 'L0_gnn_b2', 'L1_gnn_weight', 'L1_gnn_attn_l', 'L1_gnn_attn_r']


def kernel(**inputs):
    import numpy as _np
    import concourse.bacc as _bacc
    from concourse import mybir as _mybir
    from concourse.bass_utils import run_bass_kernel_spmd as _run

    nc = _bacc.Bacc("TRN2", target_bir_lowering=False, num_devices=1)
    arrays, args = {}, []
    for name in _INS:
        a = _np.ascontiguousarray(inputs[name])
        arrays[f"in_{name}"] = a
        args.append(nc.dram_tensor(f"in_{name}", a.shape, _mybir.dt.from_np(a.dtype), kind="ExternalInput").ap())
    args.append(nc.dram_tensor("out_0", (N, F), fp32, kind="ExternalOutput").ap())
    gnn_kernel(nc, *args)
    r = _run(nc, [arrays], core_ids=[0])
    return r.results[0]["out_0"]
```
